# Optimizing a Trainium2 kernel written in Bass

```python
import numpy as np
import jax
import jax.numpy as jnp

def _softmax(x, axis=-1):
    return jax.nn.softmax(x, axis=axis)

def _gelu(x):
    return jax.nn.gelu(x, approximate=True)

def _silu(x):
    return jax.nn.silu(x)

def _sigmoid(x):
    return jax.nn.sigmoid(x)

def _layernorm(x, axis=-1, eps=1e-05):
    m = jnp.mean(x, axis=axis, keepdims=True)
    v = jnp.var(x, axis=axis, keepdims=True)
    return (x - m) / jnp.sqrt(v + eps)

def _scatter_add(tgt, idx, src, axis=0):
    return tgt.at[idx].add(src)

def _segment_sum(src, seg, n):
    return jax.ops.segment_sum(src, seg, n)
kernel_name = 'mk_xattn_ffn_d2_seqx_r4_543358'

def setup_inputs(seed: int=0):
    np.random.seed(seed)
    _w = jnp.asarray

    def _rec_inputs():
        import jax
        import jax.numpy as jnp
        _rk = jax.random.key(seed)
        x = 7.22e-05 + 1 * jax.random.normal(jax.random.fold_in(_rk, 1), (8, 256, 512), jnp.float32)
        _lenS = 256 - jax.random.randint(jax.random.fold_in(_rk, 7), (8,), 0, max(1, 256 // 4) + 1, jnp.int32)
        _lenS2 = 256 - jax.random.randint(jax.random.fold_in(_rk, 8), (8,), 0, max(1, 256 // 4) + 1, jnp.int32)
        _ctx_2048P = jax.random.normal(jax.random.fold_in(_rk, 11), (8, 16, 512), jnp.float32)
        _ctx_2048c = jax.random.dirichlet(jax.random.fold_in(_rk, 511), 0.3 * jnp.ones((16,), jnp.float32), (8, 256))
        _ctx_2048t = jnp.einsum('bsk,bkd->bsd', _ctx_2048c, _ctx_2048P)
        _ctx_2048t = _ctx_2048t * jax.lax.rsqrt(jnp.mean(jnp.square(_ctx_2048t)) + 1e-12) * 0.953939
        ctx_2048 = 4.13588e-05 + 0.999923 * (_ctx_2048t + 0.3 * jax.random.normal(jax.random.fold_in(_rk, 611), (8, 256, 512), jnp.float32))
        return (x, ctx_2048)
    x, ctx_2048 = _rec_inputs()

    def _L0_xattn_setup():
        import jax, jax.numpy as jnp
        import numpy as np
        B, D, N, H = (4, 256, 512, 16)
        HD = D // H

        def rotate_half(x):
            x1 = x[..., 0::2]
            x2 = x[..., 1::2]
            return jnp.stack((-x2, x1), axis=-1).reshape(x.shape)

        def apply_cached_rotary_emb(freqs, t):
            return t * freqs[0] + rotate_half(t) * freqs[1]
        key = jax.random.key(seed)
        ks = jax.random.split(key, 13)
        s = 1.0 / np.sqrt(D)
        inp = {'query': jax.random.normal(ks[0], (B, D, N), jnp.float32), 'key': jax.random.normal(ks[1], (B, D, N), jnp.float32), 'value': jax.random.normal(ks[2], (B, D, N), jnp.float32), 'encoding': jax.random.normal(ks[3], (2, 1, 1, N, HD), jnp.float32), 'Wq': jax.random.normal(ks[4], (D, D), jnp.float32) * s, 'bq': jax.random.normal(ks[5], (D,), jnp.float32) * s, 'Wk': jax.random.normal(ks[6], (D, D), jnp.float32) * s, 'bk': jax.random.normal(ks[7], (D,), jnp.float32) * s, 'Wv': jax.random.normal(ks[8], (D, D), jnp.float32) * s, 'bv': jax.random.normal(ks[9], (D,), jnp.float32) * s, 'Wm': jax.random.normal(ks[10], (D, D), jnp.float32) * s, 'bm': jax.random.normal(ks[11], (D,), jnp.float32) * s}
        return inp
    _L0_xattn_all = _L0_xattn_setup()
    _L0_xattn_in = {k: v for k, v in _L0_xattn_all.items() if k in ('encoding', 'Wq', 'bq', 'Wk', 'bk', 'Wv', 'bv', 'Wm', 'bm')}
    del _L0_xattn_all

    def _L0_ffn_setup():
        import jax, jax.numpy as jnp
        import numpy as np
        E = 64
        K = 6
        CAP = 128
        SCALE = 1.0
        H = 512
        I = 192
        SI = I * 2
        B, S = (2, 256)

        def _moe(x, gate_w, gate_up_proj, down_proj, shared_gate_w, shared_up_w, shared_down_w):
            b, s, h = x.shape
            T = b * s
            xf = x.reshape(T, h)
            scores = jax.nn.softmax(xf @ gate_w.T, axis=-1)
            topk_w, topk_idx = jax.lax.top_k(scores, K)
            topk_w = topk_w * SCALE
            flat_e = topk_idx.reshape(-1)
            order = jnp.argsort(flat_e)
            sorted_e = flat_e[order]
            sorted_tok = (order // K).astype(jnp.int32)
            sorted_w = topk_w.reshape(-1)[order]
            counts = jnp.zeros((E,), jnp.int32).at[flat_e].add(1)
            offsets = jnp.cumsum(counts) - counts
            pos = jnp.arange(T * K, dtype=jnp.int32) - offsets[sorted_e]
            buf_tok = jnp.full((E, CAP), T, jnp.int32).at[sorted_e, pos].set(sorted_tok, mode='drop')
            buf_w = jnp.zeros((E, CAP), x.dtype).at[sorted_e, pos].set(sorted_w, mode='drop')
            xp = jnp.concatenate([xf, jnp.zeros((1, h), x.dtype)], axis=0)
            gx = xp[buf_tok]
            gu = jnp.einsum('ech,ehi->eci', gx, gate_up_proj)
            g, u = jnp.split(gu, 2, axis=-1)
            hid = jax.nn.silu(g) * u
            eo = jnp.einsum('eci,eih->ech', hid, down_proj) * buf_w[..., None]
            routed = jnp.zeros((T + 1, h), x.dtype).at[buf_tok.reshape(-1)].add(eo.reshape(-1, h))[:T]
            shared = jax.nn.silu(xf @ shared_gate_w.T) * (xf @ shared_up_w.T) @ shared_down_w.T
            return (routed + shared).reshape(b, s, h)
        key = jax.random.key(seed)
        ks = jax.random.split(key, 7)
        x = jax.random.normal(ks[0], (B, S, H), jnp.float32)
        gate_w = jax.random.normal(ks[1], (E, H), jnp.float32) * 0.02
        gate_up_proj = jax.random.normal(ks[2], (E, H, 2 * I), jnp.float32) * 0.02
        down_proj = jax.random.normal(ks[3], (E, I, H), jnp.float32) * 0.02
        shared_gate_w = jax.random.normal(ks[4], (SI, H), jnp.float32) * 0.02
        shared_up_w = jax.random.normal(ks[5], (SI, H), jnp.float32) * 0.02
        shared_down_w = jax.random.normal(ks[6], (H, SI), jnp.float32) * 0.02
        return dict(x=x, gate_w=gate_w, gate_up_proj=gate_up_proj, down_proj=down_proj, shared_gate_w=shared_gate_w, shared_up_w=shared_up_w, shared_down_w=shared_down_w)
    _L0_ffn_all = _L0_ffn_setup()
    _L0_ffn_in = {k: v for k, v in _L0_ffn_all.items() if k in ('gate_w', 'gate_up_proj', 'down_proj', 'shared_gate_w', 'shared_up_w', 'shared_down_w')}
    del _L0_ffn_all

    def _L1_xattn_setup():
        import jax, jax.numpy as jnp
        import numpy as np
        N_HEADS = 16
        K_CH = 256 // N_HEADS
        SCALE = 1.0 / np.sqrt(K_CH)
        key = jax.random.key(seed)
        ks = jax.random.split(key, 10)
        B, C, T = (4, 256, 512)
        Cout = 256
        xavier = lambda k, o, i: jax.random.uniform(k, (o, i), jnp.float32, -1.0, 1.0) * np.sqrt(6.0 / (o + i))
        return {'x': jax.random.normal(ks[0], (B, C, T), jnp.float32), 'c': jax.random.normal(ks[1], (B, C, T), jnp.float32), 'Wq': xavier(ks[2], C, C), 'bq': jnp.zeros((C,), jnp.float32), 'Wk': xavier(ks[3], C, C), 'bk': jnp.zeros((C,), jnp.float32), 'Wv': xavier(ks[4], C, C), 'bv': jnp.zeros((C,), jnp.float32), 'Wo': xavier(ks[5], Cout, C), 'bo': jnp.zeros((Cout,), jnp.float32)}
    _L1_xattn_all = _L1_xattn_setup()
    _L1_xattn_in = {k: v for k, v in _L1_xattn_all.items() if k in ('Wq', 'bq', 'Wk', 'bk', 'Wv', 'bv', 'Wo', 'bo')}
    del _L1_xattn_all

    def _L1_ffn_setup():
        import jax, jax.numpy as jnp
        import numpy as np
        TOP_K = 2
        key = jax.random.key(seed)
        ks = jax.random.split(key, 5)
        B, S, D, INTER, E = (4, 512, 512, 512, 8)
        x = jax.random.normal(ks[0], (B, S, D), dtype=jnp.float32)
        w1 = jax.random.normal(ks[1], (INTER, D), dtype=jnp.float32) * (1.0 / np.sqrt(D))
        w3 = jax.random.normal(ks[2], (INTER, INTER), dtype=jnp.float32) * (1.0 / np.sqrt(INTER))
        w2 = jax.random.normal(ks[3], (D, INTER), dtype=jnp.float32) * (1.0 / np.sqrt(INTER))
        wr = jax.random.normal(ks[4], (E, D), dtype=jnp.float32) * (1.0 / np.sqrt(D))
        return {'x': x, 'w1': w1, 'w3': w3, 'w2': w2, 'wr': wr}
    _L1_ffn_all = _L1_ffn_setup()
    _L1_ffn_in = {k: v for k, v in _L1_ffn_all.items() if k in ('w1', 'w3', 'w2', 'wr')}
    del _L1_ffn_all
    return {'x': x, 'ctx_2048': ctx_2048, 'L0_xattn_encoding': _L0_xattn_in['encoding'], 'L0_xattn_Wq': _L0_xattn_in['Wq'], 'L0_xattn_bq': _L0_xattn_in['bq'], 'L0_xattn_Wk': _L0_xattn_in['Wk'], 'L0_xattn_bk': _L0_xattn_in['bk'], 'L0_xattn_Wv': _L0_xattn_in['Wv'], 'L0_xattn_bv': _L0_xattn_in['bv'], 'L0_xattn_Wm': _L0_xattn_in['Wm'], 'L0_xattn_bm': _L0_xattn_in['bm'], 'L0_ffn_gate_w': _L0_ffn_in['gate_w'], 'L0_ffn_gate_up_proj': _L0_ffn_in['gate_up_proj'], 'L0_ffn_down_proj': _L0_ffn_in['down_proj'], 'L0_ffn_shared_gate_w': _L0_ffn_in['shared_gate_w'], 'L0_ffn_shared_up_w': _L0_ffn_in['shared_up_w'], 'L0_ffn_shared_down_w': _L0_ffn_in['shared_down_w'], 'L1_xattn_Wq': _L1_xattn_in['Wq'], 'L1_xattn_bq': _L1_xattn_in['bq'], 'L1_xattn_Wk': _L1_xattn_in['Wk'], 'L1_xattn_bk': _L1_xattn_in['bk'], 'L1_xattn_Wv': _L1_xattn_in['Wv'], 'L1_xattn_bv': _L1_xattn_in['bv'], 'L1_xattn_Wo': _L1_xattn_in['Wo'], 'L1_xattn_bo': _L1_xattn_in['bo'], 'L1_ffn_w1': _L1_ffn_in['w1'], 'L1_ffn_w3': _L1_ffn_in['w3'], 'L1_ffn_w2': _L1_ffn_in['w2'], 'L1_ffn_wr': _L1_ffn_in['wr']}

def reference(x, ctx_2048, L0_xattn_encoding, L0_xattn_Wq, L0_xattn_bq, L0_xattn_Wk, L0_xattn_bk, L0_xattn_Wv, L0_xattn_bv, L0_xattn_Wm, L0_xattn_bm, L0_ffn_gate_w, L0_ffn_gate_up_proj, L0_ffn_down_proj, L0_ffn_shared_gate_w, L0_ffn_shared_up_w, L0_ffn_shared_down_w, L1_xattn_Wq, L1_xattn_bq, L1_xattn_Wk, L1_xattn_bk, L1_xattn_Wv, L1_xattn_bv, L1_xattn_Wo, L1_xattn_bo, L1_ffn_w1, L1_ffn_w3, L1_ffn_w2, L1_ffn_wr):
    import jax
    import jax.numpy as jnp

    def _L0_xattn_ref(query, key, value, encoding, Wq, bq, Wk, bk, Wv, bv, Wm, bm):
        import jax, jax.numpy as jnp
        import numpy as np
        B, D, N, H = (4, 256, 512, 16)
        HD = D // H

        def rotate_half(x):
            x1 = x[..., 0::2]
            x2 = x[..., 1::2]
            return jnp.stack((-x2, x1), axis=-1).reshape(x.shape)

        def apply_cached_rotary_emb(freqs, t):
            return t * freqs[0] + rotate_half(t) * freqs[1]
        b, d_model, n = query.shape

        def proj(W, bias, x):
            return jnp.einsum('oi,bin->bon', W, x) + bias[None, :, None]
        q = proj(Wq, bq, query).reshape(b, HD, H, n)
        k = proj(Wk, bk, key).reshape(b, HD, H, n)
        v = proj(Wv, bv, value).reshape(b, HD, H, n)
        q = jnp.transpose(apply_cached_rotary_emb(encoding, jnp.transpose(q, (0, 2, 3, 1))), (0, 3, 1, 2))
        k = jnp.transpose(apply_cached_rotary_emb(encoding, jnp.transpose(k, (0, 2, 3, 1))), (0, 3, 1, 2))
        scores = jnp.einsum('bdhn,bdhm->bhnm', q, k) / np.float32(np.sqrt(HD))
        prob = jax.nn.softmax(scores, axis=-1)
        x = jnp.einsum('bhnm,bdhm->bdhn', prob, v)
        out = jnp.einsum('oi,bin->bon', Wm, x.reshape(b, d_model, n)) + bm[None, :, None]
        return out

    def _L0_ffn_ref(x, gate_w, gate_up_proj, down_proj, shared_gate_w, shared_up_w, shared_down_w):
        import jax, jax.numpy as jnp
        import numpy as np
        E = 64
        K = 6
        CAP = 128
        SCALE = 1.0
        H = 512
        I = 192
        SI = I * 2
        B, S = (2, 256)

        def _moe(x, gate_w, gate_up_proj, down_proj, shared_gate_w, shared_up_w, shared_down_w):
            b, s, h = x.shape
            T = b * s
            xf = x.reshape(T, h)
            scores = jax.nn.softmax(xf @ gate_w.T, axis=-1)
            topk_w, topk_idx = jax.lax.top_k(scores, K)
            topk_w = topk_w * SCALE
            flat_e = topk_idx.reshape(-1)
            order = jnp.argsort(flat_e)
            sorted_e = flat_e[order]
            sorted_tok = (order // K).astype(jnp.int32)
            sorted_w = topk_w.reshape(-1)[order]
            counts = jnp.zeros((E,), jnp.int32).at[flat_e].add(1)
            offsets = jnp.cumsum(counts) - counts
            pos = jnp.arange(T * K, dtype=jnp.int32) - offsets[sorted_e]
            buf_tok = jnp.full((E, CAP), T, jnp.int32).at[sorted_e, pos].set(sorted_tok, mode='drop')
            buf_w = jnp.zeros((E, CAP), x.dtype).at[sorted_e, pos].set(sorted_w, mode='drop')
            xp = jnp.concatenate([xf, jnp.zeros((1, h), x.dtype)], axis=0)
            gx = xp[buf_tok]
            gu = jnp.einsum('ech,ehi->eci', gx, gate_up_proj)
            g, u = jnp.split(gu, 2, axis=-1)
            hid = jax.nn.silu(g) * u
            eo = jnp.einsum('eci,eih->ech', hid, down_proj) * buf_w[..., None]
            routed = jnp.zeros((T + 1, h), x.dtype).at[buf_tok.reshape(-1)].add(eo.reshape(-1, h))[:T]
            shared = jax.nn.silu(xf @ shared_gate_w.T) * (xf @ shared_up_w.T) @ shared_down_w.T
            return (routed + shared).reshape(b, s, h)
        return _moe(x, gate_w, gate_up_proj, down_proj, shared_gate_w, shared_up_w, shared_down_w)

    def _L1_xattn_ref(x, c, Wq, bq, Wk, bk, Wv, bv, Wo, bo):
        import jax, jax.numpy as jnp
        import numpy as np
        N_HEADS = 16
        K_CH = 256 // N_HEADS
        SCALE = 1.0 / np.sqrt(K_CH)
        B, C, T = x.shape
        H, K = (N_HEADS, K_CH)
        q = jnp.einsum('oc,bct->bot', Wq, x) + bq[None, :, None]
        k = jnp.einsum('oc,bct->bot', Wk, c) + bk[None, :, None]
        v = jnp.einsum('oc,bct->bot', Wv, c) + bv[None, :, None]
        q = q.reshape(B, H, K, T)
        k = k.reshape(B, H, K, -1)
        v = v.reshape(B, H, K, -1)
        scores = jnp.einsum('bhkt,bhks->bhts', q, k) * SCALE
        p = jax.nn.softmax(scores, axis=-1)
        out = jnp.einsum('bhts,bhks->bhkt', p, v)
        out = out.reshape(B, H * K, T)
        return jnp.einsum('oc,bct->bot', Wo, out) + bo[None, :, None]

    def _L1_ffn_ref(x, w1, w3, w2, wr):
        import jax, jax.numpy as jnp
        import numpy as np
        TOP_K = 2
        B, S, D = x.shape
        xr = x.reshape(-1, D)
        route_probs = jax.nn.softmax(xr @ wr.T, axis=-1)
        routes_k, indices_k = jax.lax.top_k(route_probs, TOP_K)
        gates = routes_k / jnp.sum(routes_k, axis=-1, keepdims=True)
        h = jax.nn.silu(xr @ w1.T)
        h = jax.nn.silu(h @ w3.T)
        h = h @ w2.T
        out = jnp.zeros_like(xr)
        for k in range(TOP_K):
            out = out.at[indices_k[:, k]].add(gates[:, k:k + 1] * h)
        return out.reshape(B, S, D)
    x = x + _L0_xattn_ref(_layernorm(x, axis=-1), ctx_2048, ctx_2048, L0_xattn_encoding, L0_xattn_Wq, L0_xattn_bq, L0_xattn_Wk, L0_xattn_bk, L0_xattn_Wv, L0_xattn_bv, L0_xattn_Wm, L0_xattn_bm)
    x = x + _L0_ffn_ref(_layernorm(x, axis=-1), L0_ffn_gate_w, L0_ffn_gate_up_proj, L0_ffn_down_proj, L0_ffn_shared_gate_w, L0_ffn_shared_up_w, L0_ffn_shared_down_w)
    x = x + _L1_xattn_ref(_layernorm(x, axis=-1), ctx_2048, L1_xattn_Wq, L1_xattn_bq, L1_xattn_Wk, L1_xattn_bk, L1_xattn_Wv, L1_xattn_bv, L1_xattn_Wo, L1_xattn_bo)
    x = x + _L1_ffn_ref(_layernorm(x, axis=-1), L1_ffn_w1, L1_ffn_w3, L1_ffn_w2, L1_ffn_wr)
    return x

_drawn_inputs = setup_inputs


def setup_inputs(seed=0):
    import zlib

    import numpy as np

    out = dict(_drawn_inputs(seed))
    spreads = {'L1_xattn_bq': (0.0, 2.0),
     'L1_xattn_bk': (0.0, 2.0),
     'L1_xattn_bv': (0.0, 0.8),
     'L1_xattn_bo': (0.0, 0.8)}
    factors = {'L0_ffn_gate_w': 8.0,
     'L0_ffn_gate_up_proj': 8.0,
     'L0_ffn_down_proj': 8.0,
     'L0_ffn_shared_gate_w': 13.026,
     'L0_xattn_bv': 8.0,
     'L0_xattn_bm': 8.0,
     'L0_ffn_shared_up_w': 4.481,
     'L0_ffn_shared_down_w': 4.479,
     'L1_xattn_Wq': 3.256}
    for name, (base, spread) in spreads.items():
        noise = np.random.default_rng([zlib.crc32(name.encode()), seed]).standard_normal(out[name].shape)
        drawn = base * np.exp(spread * noise) if base else spread * noise
        out[name] = jnp.asarray(drawn.astype(out[name].dtype))
    for name, factor in factors.items():
        out[name] = (out[name] * factor).astype(out[name].dtype)
    return out
```

```python
from contextlib import ExitStack

import concourse.bass as bass
from concourse import mybir

F32 = mybir.dt.float32
BF16 = mybir.dt.bfloat16
I32 = mybir.dt.int32
U32 = mybir.dt.uint32
ALU = mybir.AluOpType
ACT = mybir.ActivationFunctionType
AX = mybir.AxisListType

B, C, N = 8, 256, 512
CT = C // 128
TILES = B * CT
H, HD = 16, 16
MT = N // 128
QUAD = 4
LEAD = 7
PARTS = ((0, 0, 1, 0, 2, 1), (0, 1, 0, 2, 0, 1))
KST = 6 * HD + 3
EPS = 1e-5


def load_rows(nc, X, mem, x):
    with ExitStack() as ctx:
        x_in = ctx.enter_context(nc.semaphore("x_in"))
        blank = ctx.enter_context(nc.semaphore("ident_blank"))
        made = ctx.enter_context(nc.semaphore("ident_made"))
        block = ctx.enter_context(nc.Block())

        @block.sync
        def _(sp):
            for b in range(B):
                sp.dma_start(X[:, CT * b:CT * (b + 1), :], x[b].rearrange("(t p) n -> p t n", p=128))\
                  .then_inc(x_in, 16)
            sp.wait_ge(x_in, 16 * B)

        @block.gpsimd
        def _(pool):
            pool.memset(mem["ident"][:], 0.0).then_inc(blank, 1)
            pool.wait_ge(blank, 1)
            pool.affine_select(out=mem["ident"][:], in_=mem["ident"][:], compare_op=ALU.not_equal, fill=1.0, base=0,
                               pattern=[[-1, 128]], channel_multiplier=1).then_inc(made, 1)
            pool.wait_ge(made, 1)
            pool.tensor_copy(mem["ident_b"][:], mem["ident"][:]).then_inc(made, 1)
            pool.memset(mem["zero"][:], 0.0).then_inc(made, 1)
            pool.wait_ge(made, 3)


def row_statistics(nc, tag, X, mem):
    mean, rstd = mem["mean"], mem["rstd"]
    with ExitStack() as ctx:
        stats = ctx.enter_context(nc.sbuf_tensor(tag + "stats", [128, TILES, 6], F32))
        moments = ctx.enter_context(nc.sbuf_tensor(tag + "moments", [128, TILES, 2], F32))
        var = ctx.enter_context(nc.sbuf_tensor(tag + "var", [128, TILES], F32))
        root = ctx.enter_context(nc.sbuf_tensor(tag + "root", [128, TILES], F32))
        err = ctx.enter_context(nc.sbuf_tensor(tag + "err", [128, TILES], F32))
        dve_chain = ctx.enter_context(nc.semaphore(tag + "ln_chain"))
        root_set = ctx.enter_context(nc.semaphore(tag + "root_set"))
        block = ctx.enter_context(nc.Block())

        @block.vector
        def _(dve):
            chained = 0

            def chain(instruction):
                nonlocal chained
                chained += 1
                instruction.then_inc(dve_chain, 1)
                dve.wait_ge(dve_chain, chained)

            for i in range(TILES):
                last = dve.bn_stats(stats[:, i, :], X[:, i, :])
            chain(last)
            for i in range(TILES):
                last = dve.bn_aggr(moments[:, i, :], stats[:, i, :])
            chain(last)
            chain(dve.tensor_scalar(var[:], moments[:, :, 1], EPS, None, ALU.add))
            chain(dve.tensor_copy(mean[:, :, 0], moments[:, :, 0]))
            dve.wait_ge(root_set, 1)
            r = rstd[:, :, 0]
            chain(dve.reciprocal(r, root[:]))
            chain(dve.tensor_tensor(err[:], r, r, ALU.mult))
            chain(dve.tensor_tensor(err[:], err[:], var[:], ALU.mult))
            chain(dve.tensor_scalar(err[:], err[:], -0.5, 1.5, ALU.mult, ALU.add))
            chain(dve.tensor_tensor(r, r, err[:], ALU.mult))

        @block.scalar
        def _(act):
            act.wait_ge(dve_chain, 3)
            nc.scalar.activation(root[:], var[:], ACT.Sqrt).then_inc(root_set, 1)


def attention(nc, tag, dram, X, mem, rotary, scale):
    ident_b, mean, rstd = mem["ident_b"], mem["mean"], mem["rstd"]
    with ExitStack() as ctx:
        def sb(name, shape, dt):
            return ctx.enter_context(nc.sbuf_tensor(tag + name, shape, dt))

        def pb(name, shape, dt):
            return ctx.enter_context(nc.psum_tensor(tag + name, shape, dt))

        def sem(name):
            return ctx.enter_context(nc.semaphore(tag + name))

        qst = [sb(f"qst{p}", [KST, H, N], BF16) for p in range(2)]
        kst = [sb(f"kst{p}", [KST, H, N], BF16) for p in range(2)]
        probs = [sb(f"probs{p}", [128, QUAD, N], F32) for p in range(2)]
        vz = [sb(f"vz{p}", [128, MT, H, 2 * HD], F32) for p in range(2)]
        wq, wk, wv, wo = (sb(n, [128, CT, C], F32) for n in ("wq", "wk", "wv", "wo"))
        biases = sb("biases", [128, 4, CT], F32)
        bo_all = sb("bo_all", [128, CT], F32)
        context = [sb(f"context{p}", [128, CT, N], F32) for p in range(2)]
        xn = sb("xn", [128, CT, N], F32)
        qf = [sb(f"qf{p}", [128, N], F32) for p in range(2)]
        parts = [sb(f"parts{p}", [128, 3, N], BF16) for p in range(2)]
        rest = sb("rest", [128, N], F32)
        if rotary:
            shuf = [sb(f"shuf{p}", [128, N], F32) for p in range(2)]
            cos_t, sin_t = sb("cos_t", [128, N], F32), sb("sin_t", [128, N], F32)
            sign = sb("sign", [128, 1], F32)
        mx = [sb(f"mx{p}", [128, 16], F32) for p in range(2)]
        mrest = sb("mrest", [128, 16], F32)
        msplit = [sb(f"msplit{p}", [128, 48], BF16) for p in range(2)]
        mrow = [sb(f"mrow{p}", [48, 128], BF16) for p in range(2)]
        u = [sb(f"u{p}", [128, N], F32) for p in range(2)]
        den = sb("den", [128, 64], F32)
        rden = sb("rden", [128, 64], F32)
        att = sb("att", [128, CT, N], F32)
        rfull = sb("rfull", [128, CT, N], F32)

        st = [pb(f"st{p}", [128, 2, N], F32) for p in range(2)]
        sc = [pb(f"sc{p}", [128, N], F32) for p in range(2)]
        o_ps = pb("o_ps", [128, N], F32)
        misc = pb("misc", [128, N], F32)

        scr = nc.dram_tensor(tag + "scr", [2, 2, 3, C, N], BF16, kind="Internal").ap()
        scr_u = nc.dram_tensor(tag + "scr_u", [2, H, 2 * HD, N], F32, kind="Internal").ap()
        scr_r = nc.dram_tensor(tag + "scr_r", [2, H, N], F32, kind="Internal").ap()

        weights_in = sem("weights_in")
        ones_set = sem("ones_set")
        ctx_in = [sem(f"ctx_in{p}") for p in range(2)]
        xn_set = sem("xn_set")
        bo_made, qk_made, v_made, o_made, t_made = (sem(n + "_made") for n in ("bo", "qk", "v", "o", "t"))
        bo_set = sem("bo_set")
        qf_set = sem("qf_set")
        shuf_set = sem("shuf_set")
        parts_set = sem("parts_set")
        parts_stored = [sem(f"parts_stored{p}") for p in range(2)]
        stacks_in = [sem(f"stacks_in{p}") for p in range(2)]
        vz_set = sem("vz_set")
        sc_set = sem("sc_set")
        max_set = sem("max_set")
        split_set = sem("split_set")
        mrow_set = sem("mrow_set")
        mrow_in = [sem(f"mrow_in{p}") for p in range(2)]
        st_set = sem("st_set")
        exp_set = sem("exp_set")
        pv_done = sem("pv_done")
        u_set = sem("u_set")
        u_stored = [sem(f"u_stored{p}") for p in range(2)]
        den_in = sem("den_in")
        num_in = sem("num_in")
        rden_set = sem("rden_set")
        rden_stored = sem("rden_stored")
        rfull_in = sem("rfull_in")
        att_set = sem("att_set")
        x_set = sem("x_set")
        dve_chain = sem("dve_chain")
        unit_chain = sem("unit_chain")
        max_chain = sem("max_chain")

        weight_dmas = 16 * (5 + (2 * 8 + 1 if rotary else 0))
        stack_dmas = 16 * 12
        QK = ["q0", "q1", "k0", "k1"]
        UNITS = [(2, "t"), (3, "v0"), (5, "v1"), (6, "t"), (8, "q0"), (9, "o0"), (10, "t"), (11, "q1"),
                 (12, "k0"), (13, "o1"), (14, "t"), (15, "k1")]
        FIRST_UNITS = [("bo", 0)] + [(n, 0) for n in QK + ["v0", "v1"]] + [(n, 1) for n in QK] + [("t", 0)]

        def has(kb, what, s=0):
            if what == "main":
                return kb < B
            if what == "qk":
                return kb + 2 < B
            if what == "v":
                return kb + 1 < B
            if what == "ahead":
                return 16 * kb + s + LEAD < 16 * B
            if what == "t":
                return (16 * kb + s + 2) // 4 < 4 * B
            return kb >= 1

        def unit_at(kb, b, s):
            name = dict(UNITS).get(s)
            if name is None or not has(kb, {"q": "qk", "k": "qk", "v": "v", "t": "t", "o": "out"}[name[0]], s):
                return None, None
            return name, {"q": b + 2, "k": b + 2, "v": b + 1, "o": b - 1, "t": 4 * b + (s + 2) // 4}[name[0]]

        def unit_before(kb, b, s):
            for at in range(s - 1, -1, -1):
                if unit_at(kb, b, at)[0]:
                    return unit_at(kb, b, at)
            if kb == 0:
                return FIRST_UNITS[-1]
            for at in range(15, -1, -1):
                if unit_at(kb - 1, b - 1, at)[0]:
                    return unit_at(kb - 1, b - 1, at)

        def over_batches(eng, body):
            for kb in range(2):
                body(kb, kb)
            with eng.Fori(1, (B - 2) // 2) as i:
                body(2, 2 * i)
                body(3, 2 * i + 1)
            for kb in range(B - 2, B + 1):
                body(kb, kb)

        def own(engine):
            engine.sem_inc(mem["passed"], 1)

        block = ctx.enter_context(nc.Block())

        @block.sync
        def _(sp):
            for t, name in ((wq, "wq"), (wk, "wk"), (wv, "wv"), (wo, "wo"), (biases, "biases")):
                sp.dma_start(t[:], dram[name]).then_inc(weights_in, 16)
            if rotary:
                for h in range(128 // HD):
                    for t, n in ((cos_t, 0), (sin_t, 1)):
                        sp.dma_start(t[h * HD:(h + 1) * HD, :], dram["enc"][n]).then_inc(weights_in, 16)
                sp.dma_start(sign[:], dram["sign"]).then_inc(weights_in, 16)

            def load_context(b, p):
                sp.dma_start(context[p][:], dram["ctx"][b].rearrange("(t p) n -> p t n", p=128))\
                  .then_inc(ctx_in[p], 16)

            def store_parts(b, p, unit):
                j = QK.index(unit)
                sp.wait_ge(parts_set, 4 * b + j + 1)
                sp.dma_start(scr[p, j // 2, :, 128 * (j % 2):128 * (j % 2 + 1), :].rearrange("s c n -> c s n"),
                             parts[j % 2][:]).then_inc(parts_stored[j % 2], 16)

            def load_stacks(b, p):
                for j in range(2):
                    sp.wait_ge(parts_stored[j], 32 * (b + 1))
                    own(sp)
                for which, dst in ((0, qst[p]), (1, kst[p])):
                    for r, part in enumerate(PARTS[which]):
                        sp.dma_start(dst[HD * r:HD * (r + 1), :, :],
                                     scr[p, which, part].rearrange("(h d) n -> d h n", d=HD))\
                          .then_inc(stacks_in[p], 16)

            def store_row_max(b, p, quad):
                sp.wait_ge(mrow_set, 4 * b + quad + 1)
                sp.dma_start(qst[p][KST - 3:KST, QUAD * quad:QUAD * (quad + 1), :]
                             .rearrange("s h (t n) -> s (h t) n", n=128),
                             mrow[quad % 2][:]).then_inc(mrow_in[quad % 2], 16)

            def store_values(b, p, quad):
                sp.wait_ge(u_set, 4 * b + quad + 1)
                sp.dma_start(scr_u[p, QUAD * quad:QUAD * (quad + 1)].rearrange("h r n -> (h r) n"),
                             u[quad % 2][:]).then_inc(u_stored[quad % 2], 16)

            load_context(0, 0)
            load_context(1, 1)
            for unit in QK:
                store_parts(0, 0, unit)
            load_stacks(0, 0)
            for unit in QK[:2]:
                store_parts(1, 1, unit)
            store_row_max(0, 0, 0)
            store_parts(1, 1, QK[2])

            def body(kb, b):
                p = kb % 2
                for s in range(16):
                    if s == 0 and has(kb, "qk"):
                        sp.wait_ge(vz_set, 2 * (b + 1))
                        load_context(b + 2, p)
                    if s == 1 and has(kb, "out"):
                        store_values(b - 1, 1 - p, 3)
                    if s in (2, 6, 10, 14) and has(kb, "t", s):
                        store_row_max(*((b, p, (s + 2) // 4) if s < 14 else (b + 1, 1 - p, 0)))
                    if s == 2 and has(kb, "v"):
                        store_parts(b + 1, 1 - p, "k1")
                        if kb >= 1:
                            sp.wait_ge(st_set, 32 * b)
                            own(sp)
                        load_stacks(b + 1, 1 - p)
                    if s == 3 and has(kb, "out"):
                        for j in range(2):
                            sp.wait_ge(u_stored[j], 32 * b)
                        if kb >= 2:
                            own(sp)
                            sp.wait_ge(rden_set, b - 1)
                            own(sp)
                            sp.wait_ge(x_set, 2 * (b - 1))
                        own(sp)
                        sp.dma_start(den[:], scr_u[1 - p, :, HD, :].rearrange("h (c f) -> h c f", f=64))\
                          .then_inc(den_in, 16)
                        for t in range(CT):
                            sp.dma_start(att[:, t, :], scr_u[1 - p, 8 * t:8 * (t + 1), 0:HD, :]).then_inc(num_in, 16)
                    if s == 4 and has(kb, "out"):
                        sp.wait_ge(rden_set, b)
                        own(sp)
                        if kb >= 2:
                            sp.wait_ge(rfull_in, 32 * (b - 1))
                            own(sp)
                        sp.dma_start(scr_r[1 - p].rearrange("h (c f) -> h c f", f=64), rden[:])\
                          .then_inc(rden_stored, 16)
                        sp.wait_ge(rden_stored, 16 * b)
                        own(sp)
                        for t in range(CT):
                            sp.dma_start(rfull[:, t, :], scr_r[1 - p, 8 * t:8 * (t + 1)].unsqueeze(1)
                                         .broadcast_to([8, HD, N])).then_inc(rfull_in, 16)
                    if s in (5, 9, 13) and has(kb, "main"):
                        if s == 5 and kb >= 1:
                            sp.wait_ge(den_in, 16 * b)
                            own(sp)
                            sp.wait_ge(num_in, 32 * b)
                            own(sp)
                        store_values(b, p, (s - 1) // 4 - 1)
                    if has(kb, "qk"):
                        if s == 10:
                            sp.wait_ge(stacks_in[p], stack_dmas // 2 * (b - p) + stack_dmas)
                            own(sp)
                        if s in (10, 13, 14):
                            store_parts(b + 2, p, QK[(10, 13, 14).index(s)])

            over_batches(sp, body)

        @block.tensor
        def _(pe):
            evacuated = {"bo": lambda b: (bo_set, 1), "t": lambda q: (mrow_set, q + 1),
                         "v": lambda b, j: (vz_set, 2 * b + j + 1), "o": lambda b, j: (x_set, 2 * b + j + 1),
                         "q": lambda b, j: (qf_set, 4 * b + j + 1), "k": lambda b, j: (qf_set, 4 * b + j + 3)}

            def bank_free(name, b):
                if name in ("bo", "t"):
                    pe.wait_ge(*evacuated[name](b))
                else:
                    pe.wait_ge(*evacuated[name[0]](b, int(name[1])))

            def unit(name, b, p):
                if name == "bo":
                    for t in range(CT):
                        for c in range(CT):
                            mm = pe.matmul(misc[:, t:t + 1], wo[:, c, 128 * t:128 * (t + 1)], biases[:, 2, c:c + 1],
                                           start=(c == 0), stop=(c == CT - 1))
                    mm.then_inc(bo_made, 1)
                elif name[0] in "qk":
                    if name[0] == "q":
                        pe.wait_ge(xn_set, b + 1)
                    else:
                        pe.wait_ge(ctx_in[p], 8 * (b - p) + 16)
                    w, src = (wq, xn) if name[0] == "q" else (wk, context[p])
                    t = int(name[1])
                    for c in range(CT):
                        mm = pe.matmul(misc[:], w[:, c, 128 * t:128 * (t + 1)], src[:, c, :],
                                       start=(c == 0), stop=(c == CT - 1))
                    mm.then_inc(qk_made, 1)
                elif name[0] == "v":
                    pe.wait_ge(ctx_in[p], 8 * (b - p) + 16)
                    for j in range(2):
                        mt = 2 * int(name[1]) + j
                        for c in range(CT):
                            mm = pe.matmul(misc[:, C * j:C * (j + 1)], context[p][:, c, 128 * mt:128 * (mt + 1)],
                                           wv[:, c, :], start=(c == 0), stop=(c == CT - 1))
                    mm.then_inc(v_made, 1)
                elif name[0] == "o":
                    pe.wait_ge(att_set, 2 * (b + 1))
                    t = int(name[1])
                    for c in range(CT):
                        mm = pe.matmul(misc[:], wo[:, c, 128 * t:128 * (t + 1)], att[:, c, :],
                                       start=(c == 0), stop=(c == CT - 1))
                    mm.then_inc(o_made, 1)

            def turn_max(q, quad):
                pe.wait_ge(split_set, q + 1)
                pe.matmul(misc[0:48, 0:128], msplit[quad % 2][:], ident_b[:], start=True, stop=True).then_inc(t_made, 1)

            def plain_scores(head, p, h, nt):
                pe.wait_ge(max_set, 4 * head + nt + 1)
                pe.matmul(sc[nt % 2][:], qst[p][0:KST - 3, h, 128 * nt:128 * (nt + 1)], kst[p][0:KST - 3, h, :],
                          start=True, stop=True).then_inc(sc_set, 1)

            def weigh(g, b, kb, p, quad, mt):
                pe.wait_ge(exp_set, 2 * g + 4)
                if mt == 0:
                    pe.wait_ge(vz_set, 2 * (b + 1))
                    if kb > 0 or quad > 0:
                        pe.wait_ge(u_set, 4 * b + quad)
                for j in range(QUAD):
                    mm = pe.matmul(o_ps[32 * j:32 * (j + 1), :], vz[p][:, mt, QUAD * quad + j, :],
                                   probs[mt % 2][:, j, :], start=(mt == 0), stop=(mt == MT - 1))
                mm.then_inc(pv_done, 1)

            pe.wait_ge(weights_in, weight_dmas)
            pe.wait_ge(ones_set, 2)
            for n, (name, b) in enumerate(FIRST_UNITS):
                if name == "t":
                    pe.wait_ge(stacks_in[0], stack_dmas)
                    for head in range(LEAD):
                        for nt in range(MT):
                            plain_scores(head, 0, head, nt)
                bank_free(*FIRST_UNITS[n - 1]) if n else None
                if name == "t":
                    turn_max(0, 0)
                else:
                    unit(name, b, b)

            def body(kb, b):
                p = kb % 2
                for s in range(16):
                    quad, mt = s // 4, s % 4
                    g = 16 * b + s
                    ahead = s + LEAD

                    def scores_ahead(nt):
                        if has(kb, "ahead", s):
                            plain_scores(16 * b + ahead, p if ahead < 16 else 1 - p, ahead % 16, nt)

                    if has(kb, "main"):
                        if mt == 0:
                            pe.wait_ge(mrow_in[quad % 2], 16 * (2 * b + quad // 2 + 1))
                        for j in range(QUAD):
                            h = QUAD * quad + j
                            if j % 2 == 0:
                                pe.wait_ge(exp_set, 2 * g + j // 2 + 1)
                            mm = pe.matmul(st[j // 2][:, j % 2, :], kst[p][:, h, 128 * mt:128 * (mt + 1)],
                                           qst[p][:, h, :], start=True, stop=True)
                            if j == 1:
                                mm.then_inc(st_set, 1)
                                if ahead == 16 and has(kb, "ahead", s):
                                    pe.wait_ge(stacks_in[1 - p], stack_dmas // 2 * (b + 1 - (1 - p)) + stack_dmas)
                                scores_ahead(0)
                            if j == 3:
                                mm.then_inc(st_set, 1)
                                scores_ahead(1)
                    if s > 0 and has(kb, "main"):
                        weigh(g - 1, b, kb, p, (s - 1) // 4, (s - 1) % 4)
                    if s == 0 and kb > 0:
                        weigh(g - 1, b - 1, kb - 1, 1 - p, 3, 3)
                    scores_ahead(2)
                    name, ub = unit_at(kb, b, s)
                    if name:
                        bank_free(*unit_before(kb, b, s))
                        if name == "t":
                            turn_max(ub, (s + 2) // 4 % 4)
                        else:
                            unit(name, ub, p if name in QK else 1 - p)
                    scores_ahead(3)

            over_batches(pe, body)

        @block.scalar
        def _(act):
            act.sem_inc(exp_set, 2)
            act.wait_ge(weights_in, weight_dmas)

            def project_out(name, b, kb):
                j = QK.index(name)
                act.wait_ge(qk_made, 4 * b + j + 1)
                if kb > 0 or j >= 2:
                    act.wait_ge(parts_set, 4 * b + j - 1)
                nc.scalar.activation(qf[j % 2][:], misc[:], ACT.Identity,
                                     bias=biases[:, j // 2, j % 2:j % 2 + 1]).then_inc(qf_set, 1)

            def values_out(name, b, kb, p):
                half = int(name[1])
                act.wait_ge(v_made, 2 * b + half + 1)
                if kb >= 2:
                    act.wait_ge(pv_done, 16 * (b - 1))
                nc.scalar.copy(vz[p][:, 2 * half:2 * half + 2, :, 0:HD],
                               misc[:].rearrange("p (t h d) -> p t h d", t=2, d=HD)).then_inc(vz_set, 1)

            act.wait_ge(ones_set, 2)
            for name, b in FIRST_UNITS:
                if name in QK:
                    project_out(name, b, b)
                elif name[0] == "v":
                    values_out(name, b, b, b)

            def body(kb, b):
                p = kb % 2
                for s in range(16):
                    quad, mt = s // 4, s % 4
                    g = 16 * b + s
                    if has(kb, "main"):
                        for half in range(2):
                            act.wait_ge(st_set, 2 * g + half + 1)
                            if half == 0 and (kb > 0 or s >= 2):
                                act.wait_ge(pv_done, g - 1)
                            nc.scalar.activation(probs[mt % 2][:, 2 * half:2 * half + 2, :], st[half][:], ACT.Exp,
                                                 scale=scale).then_inc(exp_set, 1)
                    if mt == 0 and (kb > 0 or s > 0) and (has(kb, "main") or s == 0):
                        before = quad - 1
                        act.wait_ge(pv_done, 16 * b + 4 * quad)
                        if kb > 0 or quad > 2:
                            act.wait_ge(u_stored[before % 2], 16 * (2 * b + (before - before % 2) // 2))
                        nc.scalar.copy(u[before % 2][:], o_ps[:]).then_inc(u_set, 1)
                    name, ub = unit_at(kb, b, s)
                    if name in QK:
                        project_out(name, ub, kb + 2)
                    elif name and name[0] == "v":
                        values_out(name, ub, kb + 1, 1 - p)

            if "zero" in dram:
                act.dma_start(dram["slot_rows"].rearrange("(e c) n -> c e n", c=128), dram["zero"]
                              .unsqueeze(1).broadcast_to([128, SLOTS // 128, N])).then_inc(dram["zeroed"], 16)
                act.dma_start(dram["expert_rows"][SLOTS:SLOTS + 1, :], dram["zero"][0:1, :])\
                   .then_inc(dram["zeroed"], 16)
            over_batches(act, body)

        @block.vector
        def _(dve):
            chained = 0

            def chain(instruction):
                nonlocal chained
                chained += 1
                instruction.then_inc(dve_chain, 1)
                dve.wait_ge(dve_chain, chained)

            dve.sem_inc(max_set, 2)
            for p in range(2):
                chain(dve.memset(vz[p][:, :, :, HD:2 * HD], 1.0))
                dve.memset(kst[p][KST - 3:KST, :, :], 1.0).then_inc(ones_set, 1)
            dve.wait_ge(weights_in, weight_dmas)
            if rotary:
                chain(dve.tensor_scalar(sin_t[:], sin_t[:], sign[:], None, ALU.mult))
            dve.wait_ge(bo_made, 1)
            dve.tensor_tensor(bo_all[:], misc[:, 0:CT], biases[:, 3, :], ALU.add).then_inc(bo_set, 1)

            def normalise(b, kb):
                if kb > 0:
                    dve.wait_ge(qf_set, 4 * b - 2)
                for t in range(CT):
                    i = CT * b + t
                    if t == CT - 1:
                        dve.tensor_scalar(xn[:, t, :], X[:, i, :], mean[:, i, :], rstd[:, i, :],
                                          ALU.subtract, ALU.mult).then_inc(xn_set, 1)
                    else:
                        dve.tensor_scalar(xn[:, t, :], X[:, i, :], mean[:, i, :], rstd[:, i, :],
                                          ALU.subtract, ALU.mult)

            def shuffle_unit(name, b, kb):
                j = QK.index(name)
                if rotary:
                    dve.wait_ge(qf_set, 4 * b + j + 1)
                    own(dve)
                    dve.stream_shuffle(shuf[j % 2][:], qf[j % 2][:], [n ^ 1 for n in range(32)]).then_inc(shuf_set, 1)

            def maxima(head, q, quad, mt, first):
                if mt == 0 and not first:
                    dve.wait_ge(split_set, q - 1)
                for nt in range(MT):
                    dve.wait_ge(sc_set, 4 * head + nt + 1)
                    dve.tensor_reduce(mx[quad % 2][:, 4 * mt + nt:4 * mt + nt + 1], sc[nt % 2][:], AX.X, ALU.max,
                                      negate=True).then_inc(max_set, 1)

            def max_rows(q, quad, first):
                dve.wait_ge(t_made, q + 1)
                if not first:
                    dve.wait_ge(mrow_in[quad % 2], 8 * (q - quad % 2))
                dve.tensor_copy(mrow[quad % 2][:], misc[0:48, 0:128]).then_inc(mrow_set, 1)

            normalise(0, 0)
            for j, name in enumerate(QK):
                shuffle_unit(name, 0, 0)
                dve.wait_ge(qf_set, j + 1)
                if j >= 2:
                    dve.wait_ge(parts_stored[j % 2], 16)
                q = qf[j % 2][:]
                hi, mid, lo = (parts[j % 2][:, n, :] for n in range(3))
                if rotary:
                    dve.wait_ge(shuf_set, j + 1)
                    chain(dve.tensor_tensor(shuf[j % 2][:], shuf[j % 2][:], sin_t[:], ALU.mult))
                    chain(dve.tensor_tensor(q, q, cos_t[:], ALU.mult))
                    chain(dve.tensor_tensor(q, q, shuf[j % 2][:], ALU.add))
                chain(dve.tensor_copy(hi, q))
                chain(dve.tensor_tensor(rest[:], q, hi, ALU.subtract))
                chain(dve.tensor_copy(mid, rest[:]))
                dve.tensor_tensor(lo, rest[:], mid, ALU.subtract).then_inc(parts_set, 1)
            normalise(1, 1)
            for name in QK:
                shuffle_unit(name, 1, 1)
            for head in range(LEAD):
                maxima(head, head // 4, head // 4, head % 4, True)
            max_rows(0, 0, True)

            def body(kb, b):
                p = kb % 2
                for s in range(16):
                    if has(kb, "ahead", s):
                        ahead = s + LEAD
                        maxima(16 * b + ahead, 4 * b + ahead // 4, ahead // 4, ahead % 4, kb == 0 and ahead < 8)
                    if s == 3 and has(kb, "out"):
                        dve.wait_ge(den_in, 16 * b)
                        if kb >= 2:
                            dve.wait_ge(rden_stored, 16 * (b - 1))
                        dve.reciprocal(rden[:], den[:]).then_inc(rden_set, 1)
                    if s == 7 and has(kb, "qk"):
                        normalise(b + 2, kb + 2)
                    name, ub = unit_at(kb, b, s)
                    if name == "t":
                        max_rows(ub, (s + 2) // 4, kb == 0 and s == 2)
                    elif name in QK:
                        shuffle_unit(name, ub, kb + 2)
                    elif name and name[0] == "o":
                        t = int(name[1])
                        dve.wait_ge(o_made, 2 * ub + t + 1)
                        tile = CT * ub + t
                        dve.scalar_tensor_tensor(X[:, tile, :], misc[:], bo_all[:, t:t + 1], X[:, tile, :],
                                                 ALU.add, ALU.add).then_inc(x_set, 1)

            over_batches(dve, body)

        @block.gpsimd
        def _(pool):
            chained = 6 if rotary else 3

            def rotate(name, b):
                j = QK.index(name)
                m = 4 * (b - 1) + j
                pool.wait_ge(parts_set, 4 * b + j)
                if rotary:
                    pool.wait_ge(shuf_set, 4 * b + j + 1)
                    q, sh = qf[j % 2][:], shuf[j % 2][:]
                    pool.tensor_tensor(sh, sh, sin_t[:], ALU.mult).then_inc(unit_chain, 1)
                    pool.tensor_tensor(q, q, cos_t[:], ALU.mult).then_inc(unit_chain, 1)
                    pool.wait_ge(unit_chain, chained * m + 2)
                    pool.tensor_tensor(q, q, sh, ALU.add).then_inc(unit_chain, 1)

            def split(name, b):
                j = QK.index(name)
                done = chained * (4 * (b - 1) + j) + chained - 3
                pool.wait_ge(qf_set, 4 * b + j + 1)
                if rotary:
                    pool.wait_ge(unit_chain, done)
                pool.wait_ge(parts_stored[j % 2], 16 * (2 * b + j // 2))
                q = qf[j % 2][:]
                hi, mid, lo = (parts[j % 2][:, n, :] for n in range(3))
                own(pool)
                pool.tensor_copy(hi, q).then_inc(unit_chain, 1)
                pool.wait_ge(unit_chain, done + 1)
                pool.tensor_tensor(rest[:], q, hi, ALU.subtract).then_inc(unit_chain, 1)
                pool.wait_ge(unit_chain, done + 2)
                own(pool)
                pool.tensor_copy(mid, rest[:]).then_inc(unit_chain, 1)
                pool.wait_ge(unit_chain, done + 3)
                pool.tensor_tensor(lo, rest[:], mid, ALU.subtract).then_inc(parts_set, 1)

            def split_max(q, quad, first, very_first):
                pool.wait_ge(max_set, 16 * (q + 1) + 2)
                if not first:
                    pool.wait_ge(mrow_set, q - 1)
                if not very_first:
                    pool.wait_ge(split_set, q)
                m, ms = mx[quad % 2][:], msplit[quad % 2]
                own(pool)
                pool.tensor_copy(ms[:, 0:16], m).then_inc(max_chain, 1)
                pool.wait_ge(max_chain, 3 * q + 1)
                pool.tensor_tensor(mrest[:], m, ms[:, 0:16], ALU.subtract).then_inc(max_chain, 1)
                pool.wait_ge(max_chain, 3 * q + 2)
                own(pool)
                pool.tensor_copy(ms[:, 16:32], mrest[:]).then_inc(max_chain, 1)
                pool.wait_ge(max_chain, 3 * q + 3)
                pool.tensor_tensor(ms[:, 32:48], mrest[:], ms[:, 16:32], ALU.subtract).then_inc(split_set, 1)

            pool.wait_ge(weights_in, weight_dmas)
            for name in QK[:2]:
                rotate(name, 1)
                split(name, 1)
            split_max(0, 0, True, True)
            rotate(QK[2], 1)
            split(QK[2], 1)

            def body(kb, b):
                for s in range(16):
                    if s in (1, 5, 9, 13) and has(kb, "t", s + 1):
                        quad = (s + 3) // 4
                        split_max(4 * b + quad, quad, kb == 0 and quad < 2, False)
                    if s == 0 and has(kb, "v"):
                        rotate("k1", b + 1)
                    if s == 1 and has(kb, "v"):
                        split("k1", b + 1)
                    if s in (6, 7) and has(kb, "out"):
                        t = s - 6
                        pool.wait_ge(num_in, 32 * b)
                        pool.wait_ge(rfull_in, 32 * b)
                        pool.tensor_tensor(att[:, t, :], att[:, t, :], rfull[:, t, :], ALU.mult).then_inc(att_set, 1)
                    if has(kb, "qk"):
                        for n, (turn, cut) in enumerate(((9, 10), (12, 13), (13, 14))):
                            if s == turn:
                                rotate(QK[n], b + 2)
                            if s == cut:
                                split(QK[n], b + 2)

            over_batches(pool, body)
E_N, TOP, CAP, I_N = 64, 6, 128, 192
SI = 2 * I_N
SLOTS = E_N * CAP
KT = N // 128
RING = 4
HALF = I_N // 2


class Chain:

    def __init__(self, engine, sem):
        self.engine, self.sem, self.base, self.n = engine, sem, 0, 0

    def __call__(self, instruction):
        self.n += 1
        instruction.then_inc(self.sem, 1)
        self.engine.wait_ge(self.sem, self.base + self.n)


def mixture(nc, d, X, mem):
    ident, mean, rstd = mem["ident"], mem["mean"], mem["rstd"]
    slot_rows, expert_rows = mem["slot_rows"], mem["expert_rows"]
    with ExitStack() as ctx:
        def sb(name, shape, dt):
            return ctx.enter_context(nc.sbuf_tensor("m0" + name, shape, dt))

        def pb(name, shape, dt):
            return ctx.enter_context(nc.psum_tensor("m0" + name, shape, dt))

        def sem(name):
            return ctx.enter_context(nc.semaphore("m0" + name))

        gate_w = sb("gate_w", [128, KT, E_N], F32)
        sg_w = sb("sg_w", [128, KT, SI], F32)
        su_w = sb("su_w", [128, KT, SI], F32)
        sd_w = sb("sd_w", [128, SI // 128, N], F32)
        w1 = [sb(f"w1_{r}", [128, KT, 2 * I_N], F32) for r in range(RING)]
        w2 = [sb(f"w2_{r}", [HALF, 2, N], F32) for r in range(RING)]
        xl = [sb(f"xl{p}", [128, N], F32) for p in range(2)]
        xT = [sb(f"xT{p}", [128, KT, 128], F32) for p in range(2)]
        silu = sb("silu", [128, SI], F32)
        hid = [sb(f"hid{p}", [128, SI], F32) for p in range(2)]
        before = sb("before", [128, 128], BF16)
        ones = sb("ones", [128, 128], BF16)
        first_slot = sb("first_slot", [128, E_N], F32)
        first_slot_i = sb("first_slot_i", [128, E_N], I32)
        nmax = sb("nmax", [128, 1], F32)
        total = sb("total", [128, 1], F32)
        rtotal = sb("rtotal", [128, 1], F32)
        ex = sb("ex", [128, E_N], F32)
        pp = sb("pp", [128, E_N + 8], F32)
        left = sb("left", [128, E_N + 8], F32)
        best = sb("best", [128, 8], F32)
        chosen = [sb(f"chosen{p}", [128, E_N], BF16) for p in range(2)]
        so_far = [sb(f"so_far{p}", [128, E_N], BF16) for p in range(2)]
        kept = sb("kept", [128, E_N], F32)
        weight = sb("weight", [128, E_N], F32)
        slot = sb("slot", [128, E_N], F32)
        slots8 = sb("slots8", [128, 8], F32)
        dropped = sb("dropped", [128, 8], F32)
        matches = sb("matches", [128, TOP, E_N], F32)
        index = [sb(f"index{p}", [128, 8], I32) for p in range(2)]
        all_index = sb("all_index", [128, TILES, 8], I32)
        all_weight = sb("all_weight", [128, TILES, 8], F32)
        gx = [sb(f"gx{p}", [128, N], F32) for p in range(2)]
        gxT = [sb(f"gxT{p}", [128, KT, 128], F32) for p in range(2)]
        sg = sb("sg", [128, I_N], F32)
        hx = sb("hx", [128, I_N], F32)
        hT = [sb(f"hT{p}", [HALF, 2, 128], F32) for p in range(2)]
        eo = [sb(f"eo{p}", [128, N], F32) for p in range(2)]
        got = [sb(f"got{p}", [128, TOP, N], F32) for p in range(2)]
        index_c = [sb(f"index_c{p}", [128, 8], I32) for p in range(2)]

        tp = [pb(f"tp{p}", [128, KT, 128], F32) for p in range(2)]
        wide = [pb(f"wide{p}", [128, N], F32) for p in range(2)]
        small = pb("small", [128, N], F32)
        down = [pb(f"down{p}", [128, N], F32) for p in range(2)]

        weights_in = sem("weights_in")
        experts_in = [sem(f"experts_in{r}") for r in range(RING)]
        consts_set = sem("consts_set")
        xl_set, turned, xT_set = sem("xl_set"), sem("turned"), sem("xT_set")
        logits_made, nmax_set, ex_set = sem("logits_made"), sem("nmax_set"), sem("ex_set")
        wide_made, silu_set, hid_set = sem("wide_made"), sem("silu_set"), sem("hid_set")
        chosen_set, place_made, place_read = sem("chosen_set"), sem("place_made"), sem("place_read")
        down_made, added = sem("down_made"), sem("added")
        index_set = sem("index_set")
        scattered = [sem(f"scattered{p}") for p in range(2)]
        route_chain = sem("route_chain")
        gx_in = [sem(f"gx_in{p}") for p in range(2)]
        gx_turned, gxT_set = sem("gx_turned"), sem("gxT_set")
        both_made, sg_set, hx_set = sem("both_made"), sem("sg_set"), sem("hx_set")
        hx_turned, hT_set = sem("hx_turned"), sem("hT_set")
        out_made, eo_set = sem("out_made"), sem("eo_set")
        eo_stored = [sem(f"eo_stored{p}") for p in range(2)]
        copied = sem("copied")
        got_in = [sem(f"got_in{p}") for p in range(2)]
        got_used = sem("got_used")
        add_chain = sem("add_chain")

        def own(engine):
            engine.sem_inc(mem["passed"], 1)

        ROUTE_OPS = 22
        block = ctx.enter_context(nc.Block())

        @block.sync
        def _(sp):
            for t, name in ((gate_w, "gate_w"), (sg_w, "shared_gate"), (su_w, "shared_up"), (sd_w, "shared_down")):
                sp.dma_start(t[:], d[name]).then_inc(weights_in, 16)

            def load_expert(e, r):
                sp.dma_start(w1[r][:], d["gate_up"][e].rearrange("(p t) i -> p t i", t=KT)).then_inc(experts_in[r], 16)
                sp.dma_start(w2[r][:], d["down"][e].rearrange("(p t) n -> p t n", t=2)).then_inc(experts_in[r], 16)

            def load_tokens(e, p):
                sp.dma_start(gx[p][:], slot_rows[CAP * e:CAP * (e + 1), :] if isinstance(e, int)
                             else slot_rows[bass.ds(CAP * e, CAP), :]).then_inc(gx_in[p], 16)

            for r in range(RING):
                load_expert(r, r)
            for p in range(2):
                sp.wait_ge(scattered[p], 16 * TOP * TILES // 2)
            for p in range(2):
                load_tokens(p, p)

            def expert(e, r, weights, tokens):
                if tokens:
                    sp.wait_ge(gx_turned, e + 1)
                    own(sp)
                    load_tokens(e + 2, r % 2)
                if weights:
                    sp.wait_ge(out_made, e + 1)
                    own(sp)
                    load_expert(e + RING, r)

            with sp.Fori(0, E_N // RING - 1) as i:
                for r in range(RING):
                    expert(RING * i + r, r, True, True)
            for r in range(RING):
                expert(E_N - RING + r, r, False, r < RING - 2)

        @block.tensor
        def _(pe):
            pe.wait_ge(weights_in, 64)
            pe.wait_ge(consts_set, 3)

            def turn(t, p, first):
                pe.wait_ge(xl_set, t + 1)
                if not first:
                    pe.wait_ge(xT_set, t - 1)
                for k in range(KT):
                    mm = pe.transpose(tp[p][:, k, :], xl[p][:, 128 * k:128 * (k + 1)], ident[:])
                mm.then_inc(turned, 1)

            def shared_down(t, kt, p):
                pe.wait_ge(hid_set, t + 1)
                if kt >= 1:
                    pe.wait_ge(added, t)
                for k in range(SI // 128):
                    mm = pe.matmul(down[p][:], hid[p][:, 128 * k:128 * (k + 1)], sd_w[:, k, :],
                                   start=(k == 0), stop=(k == SI // 128 - 1))
                mm.then_inc(down_made, 1)

            def tile(kt, t):
                p = kt % 2
                pe.wait_ge(xT_set, t + 1)
                if kt > 0:
                    pe.wait_ge(place_read, t)
                for k in range(KT):
                    mm = pe.matmul(small[:, 0:E_N], xT[p][:, k, :], gate_w[:, k, :], start=(k == 0), stop=(k == KT - 1))
                mm.then_inc(logits_made, 1)
                if kt > 0:
                    pe.wait_ge(hid_set, t)
                for n, w in enumerate((sg_w, su_w)):
                    for m in range(SI // 128):
                        for k in range(KT):
                            mm = pe.matmul(wide[n][:, 128 * m:128 * (m + 1)], w[:, k, 128 * m:128 * (m + 1)],
                                           xT[p][:, k, :], start=(k == 0), stop=(k == KT - 1))
                    mm.then_inc(wide_made, 1)
                if kt < TILES - 1:
                    turn(t + 1, 1 - p, kt == 0)
                if kt > 0:
                    shared_down(t - 1, kt - 1, 1 - p)
                pe.wait_ge(chosen_set, t + 1)
                pe.matmul(small[:, E_N:2 * E_N], before[:], chosen[p][:], start=True, stop=False)
                pe.matmul(small[:, E_N:2 * E_N], ones[:], so_far[p][:], start=False, stop=True).then_inc(place_made, 1)

            turn(0, 0, True)
            for t in range(2):
                tile(t, t)
            with pe.Fori(1, TILES // 2 - 1) as i:
                for p in range(2):
                    tile(2 + p, 2 * i + p)
            for t in range(TILES - 2, TILES):
                tile(t, t)
            shared_down(TILES - 1, TILES - 1, 1)

            def turn_tokens(e, ke, p):
                pe.wait_ge(gx_in[p], 8 * (e - p) + 16)
                if ke >= 2:
                    pe.wait_ge(gxT_set, e - 1)
                for k in range(KT):
                    mm = pe.transpose(tp[p][:, k, :], gx[p][:].rearrange("c (h t) -> c t h", t=KT)[:, k, :], ident[:])
                mm.then_inc(gx_turned, 1)

            def out_of(e, ke, r):
                p = r % 2
                pe.wait_ge(hT_set, e + 1)
                if ke >= 2:
                    pe.wait_ge(eo_set, e - 1)
                for t in range(2):
                    mm = pe.matmul(down[p][:], hT[p][:, t, :], w2[r][:, t, :], start=(t == 0), stop=(t == 1))
                mm.then_inc(out_made, 1)

            def expert(e, ke, r):
                p = r % 2
                pe.wait_ge(experts_in[r], 32 // RING * (e - r) + 32)
                pe.wait_ge(gxT_set, e + 1)
                if ke >= 2:
                    pe.wait_ge(hx_set, e - 1)
                for k in range(KT):
                    mm = pe.matmul(wide[p][:, 0:2 * I_N], gxT[p][:, k, :], w1[r][:, k, :],
                                   start=(k == 0), stop=(k == KT - 1))
                mm.then_inc(both_made, 1)
                if ke < E_N - 1:
                    turn_tokens(e + 1, ke + 1, 1 - p)
                if ke > 0:
                    out_of(e - 1, ke - 1, (r - 1) % RING)
                pe.wait_ge(hx_set, e + 1)
                if ke > 0:
                    pe.wait_ge(hT_set, e)
                for t in range(2):
                    mm = pe.transpose(small[0:HALF, 128 * t:128 * (t + 1)],
                                      hx[:].rearrange("c (i t) -> c t i", t=2)[:, t, :], ident[:])
                mm.then_inc(hx_turned, 1)

            pe.wait_ge(added, TILES + 1)
            pe.wait_ge(place_read, TILES)
            turn_tokens(0, 0, 0)
            for e in range(RING):
                expert(e, e, e)
            with pe.Fori(1, E_N // RING - 1) as i:
                for r in range(RING):
                    expert(RING * i + r, RING + r, r)
            for r in range(RING):
                expert(E_N - RING + r, E_N - RING + r, r)
            out_of(E_N - 1, E_N - 1, RING - 1)

        @block.scalar
        def _(act):
            def turned_out(t, p):
                act.wait_ge(turned, t + 1)
                nc.scalar.copy(xT[p][:], tp[p][:]).then_inc(xT_set, 1)

            def tile(kt, t):
                p = kt % 2
                act.wait_ge(nmax_set, t + 1)
                nc.scalar.activation(ex[:], small[:, 0:E_N], ACT.Exp, bias=nmax[:], accum_out=total[:])\
                  .then_inc(ex_set, 1)
                act.wait_ge(wide_made, 2 * t + 1)
                if kt > 0:
                    act.wait_ge(hid_set, t)
                nc.scalar.activation(silu[:], wide[0][:, 0:SI], ACT.Silu).then_inc(silu_set, 1)
                if kt < TILES - 1:
                    if kt > 0:
                        act.wait_ge(wide_made, 2 * t)
                    turned_out(t + 1, 1 - p)

            turned_out(0, 0)
            for t in range(2):
                tile(t, t)
            with act.Fori(1, TILES // 2 - 1) as i:
                for p in range(2):
                    tile(2 + p, 2 * i + p)
            for t in range(TILES - 2, TILES):
                tile(t, t)

            def tokens_out(e, ke, p):
                act.wait_ge(gx_turned, e + 1)
                if ke >= 2:
                    act.wait_ge(both_made, e - 1)
                nc.scalar.copy(gxT[p][:], tp[p][:]).then_inc(gxT_set, 1)

            def expert(e, ke, p):
                act.wait_ge(both_made, e + 1)
                if ke > 0:
                    act.wait_ge(hx_set, e)
                nc.scalar.activation(sg[:], wide[p][:, 0:I_N], ACT.Silu).then_inc(sg_set, 1)
                if ke < E_N - 1:
                    tokens_out(e + 1, ke + 1, 1 - p)

            tokens_out(0, 0, 0)
            for e in range(2):
                expert(e, e, e)
            with act.Fori(1, E_N // 2 - 1) as i:
                for p in range(2):
                    expert(2 * i + p, 2 + p, p)
            for p in range(2):
                expert(E_N - 2 + p, E_N - 2 + p, p)

        @block.vector
        def _(dve):
            chain = Chain(dve, route_chain)
            dve.sem_inc(added, 1)

            def normalise(t, kt, p):
                if kt >= 2:
                    dve.wait_ge(turned, t - 1)
                    dve.wait_ge(scattered[p], 8 * TOP * (t - p))
                dve.tensor_scalar(xl[p][:], X[:, t, :], mean[:, t, :], rstd[:, t, :],
                                  ALU.subtract, ALU.mult).then_inc(xl_set, 1)

            def add_shared(t, p):
                dve.wait_ge(down_made, t + 1)
                dve.tensor_tensor(X[:, t, :], down[p][:], X[:, t, :], ALU.add).then_inc(added, 1)

            def tile(kt, t):
                p = kt % 2
                chain.base, chain.n = 3 + ROUTE_OPS * t, 0
                dve.wait_ge(logits_made, t + 1)
                dve.tensor_reduce(nmax[:], small[:, 0:E_N], AX.X, ALU.max, negate=True).then_inc(nmax_set, 1)
                if kt < TILES - 1:
                    normalise(t + 1, kt + 1, 1 - p)
                dve.wait_ge(ex_set, t + 1)
                chain(dve.reciprocal(rtotal[:], total[:]))
                chain(dve.tensor_scalar(pp[:, 0:E_N], ex[:], rtotal[:], None, ALU.mult))
                own(dve)
                chain(dve.max(best[:], pp[:]))
                chain(dve.memset(best[:, TOP:8], -1.0))
                own(dve)
                chain(dve.match_replace(left[:], best[:], pp[:], -2.0))
                if kt >= 2:
                    dve.wait_ge(place_made, t - 1)
                chain(dve.tensor_scalar(chosen[p][:], left[:, 0:E_N], -2.0, None, ALU.is_equal))
                dve.tensor_tensor(so_far[1 - p][:], so_far[p][:], chosen[p][:], ALU.add).then_inc(chosen_set, 1)
                chain(dve.tensor_tensor(weight[:], pp[:, 0:E_N], chosen[p][:], ALU.mult))
                dve.wait_ge(silu_set, t + 1)
                dve.wait_ge(wide_made, 2 * t + 2)
                if kt >= 2:
                    dve.wait_ge(down_made, t - 1)
                dve.tensor_tensor(hid[p][:], wide[1][:, 0:SI], silu[:], ALU.mult).then_inc(hid_set, 1)
                if kt > 0:
                    add_shared(t - 1, 1 - p)
                dve.wait_ge(place_made, t + 1)
                place = small[:, E_N:2 * E_N]
                chain(dve.scalar_tensor_tensor(kept[:], place, float(CAP), chosen[p][:], ALU.is_lt, ALU.mult))
                chain(dve.tensor_tensor(slot[:], place, first_slot[:], ALU.add))
                dve.sem_inc(place_read, 1)
                chain(dve.tensor_tensor(slot[:], slot[:], kept[:], ALU.mult))
                chain(dve.tensor_tensor(weight[:], weight[:], kept[:], ALU.mult))
                own(dve)
                chain(dve.max(slots8[:], slot[:]))
                chain(dve.tensor_scalar(dropped[:], slots8[:], 0.0, float(SLOTS + 1), ALU.is_equal, ALU.mult))
                chain(dve.scalar_tensor_tensor(dropped[:], slots8[:], -1.0, dropped[:], ALU.add, ALU.add))
                if kt >= 2:
                    dve.wait_ge(scattered[p], 8 * TOP * (t - p))
                dve.tensor_copy(index[p][:], dropped[:]).then_inc(index_set, 1)
                chain(dve.tensor_copy(all_index[:, t, :], dropped[:]))
                for k in range(TOP):
                    chain(dve.scalar_tensor_tensor(matches[:, k, :], slot[:], slots8[:, k:k + 1], weight[:],
                                                   ALU.is_equal, ALU.mult))
                chain(dve.tensor_reduce(all_weight[:, t, 0:TOP], matches[:], AX.X, ALU.add))
                assert chain.n == ROUTE_OPS, chain.n

            chain(dve.memset(pp[:, E_N:E_N + 8], -1.0))
            chain(dve.memset(so_far[0][:], 0.0))
            dve.wait_ge(consts_set, 3)
            chain(dve.tensor_copy(first_slot[:], first_slot_i[:]))
            normalise(0, 0, 0)
            for t in range(2):
                tile(t, t)
            with dve.Fori(1, TILES // 2 - 1) as i:
                for p in range(2):
                    tile(2 + p, 2 * i + p)
            for t in range(TILES - 2, TILES):
                tile(t, t)
            add_shared(TILES - 1, 1)

            def expert_out(e, ke, p):
                dve.wait_ge(out_made, e + 1)
                if ke >= 2:
                    dve.wait_ge(eo_stored[p], 8 * (e - p))
                dve.tensor_copy(eo[p][:], down[p][:]).then_inc(eo_set, 1)

            def expert(e, ke, p):
                dve.wait_ge(sg_set, e + 1)
                if ke > 0:
                    dve.wait_ge(hx_turned, e)
                dve.tensor_tensor(hx[:], wide[p][:, I_N:2 * I_N], sg[:], ALU.mult).then_inc(hx_set, 1)
                if ke > 0:
                    expert_out(e - 1, ke - 1, 1 - p)
                dve.wait_ge(hx_turned, e + 1)
                if ke >= 2:
                    dve.wait_ge(out_made, e - 1)
                dve.tensor_copy(hT[p][:], small[0:HALF, 0:256].rearrange("i (t c) -> i t c", t=2)).then_inc(hT_set, 1)

            for e in range(3):
                expert(e, e, e % 2)
            with dve.Fori(1, E_N // 2 - 1) as i:
                for p in range(2):
                    expert(2 * i + 1 + p, 3 + p, 1 - p)
            expert(E_N - 1, E_N - 1, 1)
            expert_out(E_N - 1, E_N - 1, 1)

            def combine(t, p):
                for k in range(TOP):
                    if k == 0:
                        dve.wait_ge(got_in[p], 8 * TOP * (t - p) + 16 * TOP)
                    dve.scalar_tensor_tensor(X[:, t, :], got[p][:, k, :], all_weight[:, t, k:k + 1], X[:, t, :],
                                             ALU.mult, ALU.add).then_inc(add_chain, 1)
                    dve.wait_ge(add_chain, TOP * t + k + 1)

            with dve.Fori(0, TILES // 2) as i:
                for p in range(2):
                    combine(2 * i + p, p)

        @block.gpsimd
        def _(pool):
            pool.memset(ones[:], 1.0).then_inc(consts_set, 1)
            pool.wait_ge(consts_set, 1)
            pool.affine_select(out=before[:], in_=ones[:], compare_op=ALU.is_gt, fill=0.0, base=0,
                               pattern=[[1, 128]], channel_multiplier=-1).then_inc(consts_set, 1)
            pool.iota(first_slot_i[:], pattern=[[CAP, E_N]], base=1, channel_multiplier=0).then_inc(consts_set, 1)
            pool.wait_ge(mem["zeroed"], 32)

            def scatter(t, p):
                pool.wait_ge(index_set, t + 1)
                own(pool)
                for k in range(TOP):
                    pool.indirect_dma_start(out=slot_rows, out_offset=bass.IndirectOffsetOnAxis(
                        index[p][:, k:k + 1].bitcast(U32), 0), in_=xl[p][:], in_offset=None,
                        bounds_check=SLOTS - 1, oob_is_err=False).then_inc(scattered[p], 16)

            with pool.Fori(0, TILES // 2) as i:
                for p in range(2):
                    scatter(2 * i + p, p)

            with pool.Fori(0, E_N // 2) as i:
                for p in range(2):
                    e = 2 * i + p
                    pool.wait_ge(eo_set, e + 1)
                    own(pool)
                    pool.dma_start(expert_rows[bass.ds(CAP * e, CAP), :], eo[p][:]).then_inc(eo_stored[p], 16)
            for p in range(2):
                pool.wait_ge(eo_stored[p], 16 * E_N // 2)

            def gather(t, kt, p):
                if kt >= 2:
                    pool.wait_ge(add_chain, TOP * (t - 1))
                pool.tensor_copy(index_c[p][:], all_index[:, t, :]).then_inc(copied, 1)
                pool.wait_ge(copied, t + 1)
                own(pool)
                for k in range(TOP):
                    pool.indirect_dma_start(out=got[p][:, k, :], out_offset=None, in_=expert_rows,
                                            in_offset=bass.IndirectOffsetOnAxis(
                                                index_c[p][:, k:k + 1].bitcast(U32), 0)).then_inc(got_in[p], 16)

            for p in range(2):
                gather(p, p, p)
            with pool.Fori(1, TILES // 2) as i:
                for p in range(2):
                    gather(2 * i + p, 2 + p, p)


R_N, R_TOP = 8, 2


def routed_sum(nc, d, X, mem):
    ident, mean, rstd = mem["ident"], mem["mean"], mem["rstd"]
    with ExitStack() as ctx:
        def sb(name, shape, dt):
            return ctx.enter_context(nc.sbuf_tensor("m1" + name, shape, dt))

        def pb(name, shape, dt):
            return ctx.enter_context(nc.psum_tensor("m1" + name, shape, dt))

        def sem(name):
            return ctx.enter_context(nc.semaphore("m1" + name))

        w1, w3, w2 = (sb(n, [128, KT, N], F32) for n in ("w1", "w3", "w2"))
        wr = sb("wr", [128, KT, R_N], F32)
        xl = [sb(f"xl{p}", [128, N], F32) for p in range(2)]
        xT = [sb(f"xT{p}", [128, KT, 128], F32) for p in range(2)]
        h1 = [sb(f"h1{p}", [128, KT, 128], F32) for p in range(2)]
        h2 = [sb(f"h2{p}", [128, N], F32) for p in range(2)]
        nmax, total, rtotal, gsum = (sb(n, [128, 1], F32) for n in ("nmax", "total", "rtotal", "gsum"))
        ex = sb("ex", [128, R_N], F32)
        pp, left = sb("pp", [128, 2 * R_N], F32), sb("left", [128, 2 * R_N], F32)
        best = sb("best", [128, 8], F32)
        gates = [sb(f"gates{p}", [128, R_N], F32) for p in range(2)]
        summed = sb("summed", [R_N, N], F32)
        summedT = sb("summedT", [128, KT, R_N], F32)

        tp = [pb(f"tp{p}", [128, KT, 128], F32) for p in range(2)]
        first = [pb(f"first{p}", [128, KT, 128], F32) for p in range(2)]
        second = [pb(f"second{p}", [128, N], F32) for p in range(2)]
        small = pb("small", [128, N], F32)
        acc = pb("acc", [R_N, N], F32)

        weights_in = sem("weights_in")
        xl_set, turned, xT_set = sem("xl_set"), sem("turned"), sem("xT_set")
        logits_made, nmax_set, ex_set, gates_set = sem("logits_made"), sem("nmax_set"), sem("ex_set"), sem("gates_set")
        first_made, h1_set, second_made, h2_set = sem("first_made"), sem("h1_set"), sem("second_made"), sem("h2_set")
        gathered = sem("gathered")
        summed_set, summed_turned, summedT_set, last_made = (
            sem(n) for n in ("summed_set", "summed_turned", "summedT_set", "last_made"))
        gate_chain = sem("gate_chain")
        def own(engine):
            engine.sem_inc(mem["passed"], 1)

        GATE_OPS = 9
        block = ctx.enter_context(nc.Block())

        def over_tiles(eng, tile):
            for t in range(2):
                tile(t, t)
            with eng.Fori(1, TILES // 2 - 1) as i:
                for p in range(2):
                    tile(2 + p, 2 * i + p)
            for t in range(TILES - 2, TILES):
                tile(t, t)

        @block.sync
        def _(sp):
            for t, name in ((wr, "wr"), (w1, "w1"), (w3, "w3"), (w2, "w2")):
                sp.dma_start(t[:], d[name]).then_inc(weights_in, 16)

        @block.tensor
        def _(pe):
            def turn(t, kt, p):
                pe.wait_ge(xl_set, t + 1)
                if kt >= 2:
                    pe.wait_ge(xT_set, t - 1)
                for k in range(KT):
                    mm = pe.transpose(tp[p][:, k, :], xl[p][:, 128 * k:128 * (k + 1)], ident[:])
                mm.then_inc(turned, 1)

            def second_of(t, kt, p):
                pe.wait_ge(h1_set, t + 1)
                if kt >= 2:
                    pe.wait_ge(h2_set, t - 1)
                for k in range(KT):
                    mm = pe.matmul(second[p][:], h1[p][:, k, :], w3[:, k, :], start=(k == 0), stop=(k == KT - 1))
                mm.then_inc(second_made, 1)

            def gather(t, p, start, stop):
                pe.wait_ge(h2_set, t + 1)
                pe.wait_ge(gates_set, t + 1)
                pe.matmul(acc[:], gates[p][:], h2[p][:], start=start, stop=stop).then_inc(gathered, 1)

            def tile(kt, t):
                p = kt % 2
                pe.wait_ge(xT_set, t + 1)
                if kt > 0:
                    pe.wait_ge(ex_set, t)
                for k in range(KT):
                    mm = pe.matmul(small[:, 0:R_N], xT[p][:, k, :], wr[:, k, :], start=(k == 0), stop=(k == KT - 1))
                mm.then_inc(logits_made, 1)
                if kt >= 2:
                    pe.wait_ge(h1_set, t - 1)
                for m in range(KT):
                    for k in range(KT):
                        mm = pe.matmul(first[p][:, m, :], w1[:, k, 128 * m:128 * (m + 1)], xT[p][:, k, :],
                                       start=(k == 0), stop=(k == KT - 1))
                mm.then_inc(first_made, 1)
                if kt < TILES - 1:
                    turn(t + 1, kt + 1, 1 - p)
                if kt >= 1:
                    second_of(t - 1, kt - 1, 1 - p)
                if kt >= 2:
                    gather(t - 2, p, kt == 2, False)

            pe.wait_ge(weights_in, 64)
            turn(0, 0, 0)
            for t in range(3):
                tile(t, t)
            with pe.Fori(1, TILES // 2 - 1) as i:
                for p in range(2):
                    tile(3 + p, 2 * i + 1 + p)
            tile(TILES - 1, TILES - 1)
            second_of(TILES - 1, TILES - 1, 1)
            gather(TILES - 2, 0, False, False)
            gather(TILES - 1, 1, False, True)
            pe.wait_ge(summed_set, 1)
            for k in range(KT):
                mm = pe.transpose(small[:, 64 + R_N * k:64 + R_N * (k + 1)], summed[:, 128 * k:128 * (k + 1)],
                                  ident[0:R_N, 0:R_N])
            mm.then_inc(summed_turned, 1)
            pe.wait_ge(summedT_set, 1)
            for k in range(KT):
                mm = pe.matmul(acc[:], summedT[:, k, :], w2[:, k, :], start=(k == 0), stop=(k == KT - 1))
            mm.then_inc(last_made, 1)

        @block.scalar
        def _(act):
            def turned_out(t, kt, p):
                act.wait_ge(turned, t + 1)
                if kt >= 2:
                    act.wait_ge(first_made, t - 1)
                nc.scalar.copy(xT[p][:], tp[p][:]).then_inc(xT_set, 1)

            def second_out(t, kt, p):
                act.wait_ge(second_made, t + 1)
                if kt >= 2:
                    act.wait_ge(gathered, t - 1)
                nc.scalar.activation(h2[p][:], second[p][:], ACT.Silu).then_inc(h2_set, 1)

            def tile(kt, t):
                p = kt % 2
                act.wait_ge(nmax_set, t + 1)
                nc.scalar.activation(ex[:], small[:, 0:R_N], ACT.Exp, bias=nmax[:], accum_out=total[:])\
                  .then_inc(ex_set, 1)
                act.wait_ge(first_made, t + 1)
                if kt >= 2:
                    act.wait_ge(second_made, t - 1)
                nc.scalar.activation(h1[p][:], first[p][:], ACT.Silu).then_inc(h1_set, 1)
                if kt < TILES - 1:
                    turned_out(t + 1, kt + 1, 1 - p)
                if kt >= 1:
                    second_out(t - 1, kt - 1, 1 - p)

            turned_out(0, 0, 0)
            for t in range(3):
                tile(t, t)
            with act.Fori(1, TILES // 2 - 1) as i:
                for p in range(2):
                    tile(3 + p, 2 * i + 1 + p)
            tile(TILES - 1, TILES - 1)
            second_out(TILES - 1, TILES - 1, 1)

        @block.vector
        def _(dve):
            chain = Chain(dve, gate_chain)

            def normalise(t, kt, p):
                if kt >= 2:
                    dve.wait_ge(turned, t - 1)
                dve.tensor_scalar(xl[p][:], X[:, t, :], mean[:, t, :], rstd[:, t, :],
                                  ALU.subtract, ALU.mult).then_inc(xl_set, 1)

            def tile(kt, t):
                p = kt % 2
                chain.base, chain.n = 1 + GATE_OPS * t, 0
                dve.wait_ge(logits_made, t + 1)
                dve.tensor_reduce(nmax[:], small[:, 0:R_N], AX.X, ALU.max, negate=True).then_inc(nmax_set, 1)
                if kt < TILES - 1:
                    normalise(t + 1, kt + 1, 1 - p)
                dve.wait_ge(ex_set, t + 1)
                chain(dve.reciprocal(rtotal[:], total[:]))
                chain(dve.tensor_scalar(pp[:, 0:R_N], ex[:], rtotal[:], None, ALU.mult))
                own(dve)
                chain(dve.max(best[:], pp[:]))
                chain(dve.memset(best[:, R_TOP:8], -1.0))
                own(dve)
                chain(dve.match_replace(left[:], best[:], pp[:], -2.0))
                chain(dve.tensor_scalar(left[:, 0:R_N], left[:, 0:R_N], -2.0, None, ALU.is_equal))
                chain(dve.tensor_tensor(left[:, 0:R_N], left[:, 0:R_N], pp[:, 0:R_N], ALU.mult))
                chain(dve.tensor_reduce(gsum[:], left[:, 0:R_N], AX.X, ALU.add))
                chain(dve.reciprocal(gsum[:], gsum[:]))
                if kt >= 2:
                    dve.wait_ge(gathered, t - 1)
                dve.tensor_scalar(gates[p][:], left[:, 0:R_N], gsum[:], None, ALU.mult).then_inc(gates_set, 1)
                assert chain.n == GATE_OPS, chain.n

            chain(dve.memset(pp[:, R_N:2 * R_N], -1.0))
            normalise(0, 0, 0)
            over_tiles(dve, tile)
            dve.wait_ge(gathered, TILES)
            dve.tensor_copy(summed[:], acc[:]).then_inc(summed_set, 1)
            dve.wait_ge(summed_turned, 1)
            dve.tensor_copy(summedT[:], small[:, 64:64 + R_N * KT].rearrange("p (k r) -> p k r", k=KT))\
               .then_inc(summedT_set, 1)
            dve.wait_ge(last_made, 1)
            chain.base, chain.n = 1 + GATE_OPS * TILES, 0
            chain(dve.tensor_tensor(X[0:R_N, 0, :], acc[:], X[0:R_N, 0, :], ALU.add))


def program(nc, d, out, stages=(1, 2, 3, 4)):
    with ExitStack() as ctx:
        X = ctx.enter_context(nc.sbuf_tensor("X", [128, TILES, N], F32))
        mem = {
            "ident": ctx.enter_context(nc.sbuf_tensor("ident", [128, 128], F32)),
            "ident_b": ctx.enter_context(nc.sbuf_tensor("ident_b", [128, 128], BF16)),
            "mean": ctx.enter_context(nc.sbuf_tensor("mean", [128, TILES, 1], F32)),
            "rstd": ctx.enter_context(nc.sbuf_tensor("rstd", [128, TILES, 1], F32)),
        }
        mem["slot_rows"] = nc.dram_tensor("slot_rows", [SLOTS, N], F32, kind="Internal").ap()
        mem["expert_rows"] = nc.dram_tensor("expert_rows", [SLOTS + 1, N], F32, kind="Internal").ap()
        mem["passed"] = ctx.enter_context(nc.semaphore("passed"))
        mem["zeroed"] = ctx.enter_context(nc.semaphore("zeroed"))
        mem["zero"] = ctx.enter_context(nc.sbuf_tensor("zero", [128, N], F32))
        load_rows(nc, X, mem, d["x"])
        if 1 in stages:
            row_statistics(nc, "a0", X, mem)
            attention(nc, "a0", {**{k: d["L0_" + k] for k in ("wq", "wk", "wv", "wo", "biases")},
                                 "ctx": d["ctx_2048"], "enc": d["enc"], "sign": d["sign"],
                                 **({"slot_rows": mem["slot_rows"], "expert_rows": mem["expert_rows"],
                                 "zero": mem["zero"][:], "zeroed": mem["zeroed"]} if 2 in stages else {})}, X, mem, True, 0.25)
        if 2 in stages:
            row_statistics(nc, "m0", X, mem)
            mixture(nc, d, X, mem)
        if 3 in stages:
            row_statistics(nc, "a1", X, mem)
            attention(nc, "a1", {**{k: d["L1_" + k] for k in ("wq", "wk", "wv", "wo", "biases")},
                                 "ctx": d["ctx_2048"]}, X, mem, False, 0.25)
        if 4 in stages:
            row_statistics(nc, "m1", X, mem)
            routed_sum(nc, d, X, mem)
        store_rows(nc, X, out)


def store_rows(nc, X, out):
    with ExitStack() as ctx:
        x_out = ctx.enter_context(nc.semaphore("x_out"))
        block = ctx.enter_context(nc.Block())

        @block.sync
        def _(sp):
            for b in range(B):
                sp.dma_start(out[b].rearrange("(t p) n -> p t n", p=128), X[:, CT * b:CT * (b + 1), :])\
                  .then_inc(x_out, 16)
            sp.wait_ge(x_out, 16 * B)


def laid_out(inputs):
    import numpy as np

    a = {k: np.asarray(v) for k, v in inputs.items()}

    def tiles(w):
        return np.ascontiguousarray(w.reshape(-1, 128, w.shape[1]).transpose(1, 0, 2))

    def by_head(w):
        return w.reshape(HD, H, *w.shape[1:]).swapaxes(0, 1).reshape(w.shape)

    d = {"x": a["x"], "ctx_2048": a["ctx_2048"]}
    for layer, last, order in (("L0", "m", by_head), ("L1", "o", lambda w: w)):
        for n in "qkv":
            d[f"{layer}_w{n}"] = tiles(order(a[f"{layer}_xattn_W{n}"]).T)
        d[f"{layer}_wo"] = tiles(order(a[f"{layer}_xattn_W{last}"].T))
        vectors = [order(a[f"{layer}_xattn_b{n}"]) for n in "qkv"] + [a[f"{layer}_xattn_b{last}"]]
        d[f"{layer}_biases"] = np.ascontiguousarray(np.stack([v.reshape(CT, 128) for v in vectors]).transpose(2, 0, 1))
    d["enc"] = np.ascontiguousarray(a["L0_xattn_encoding"][:, 0, 0].transpose(0, 2, 1))
    d["sign"] = np.where(np.arange(128) % 2 == 0, -1.0, 1.0).astype(np.float32).reshape(128, 1)
    d["gate_w"] = tiles(a["L0_ffn_gate_w"].T)
    d["gate_up"] = a["L0_ffn_gate_up_proj"]
    d["down"] = a["L0_ffn_down_proj"]
    d["shared_gate"] = tiles(a["L0_ffn_shared_gate_w"].T)
    d["shared_up"] = tiles(a["L0_ffn_shared_up_w"].T)
    d["shared_down"] = tiles(a["L0_ffn_shared_down_w"].T)
    d["w1"] = tiles(a["L1_ffn_w1"].T)
    d["w3"] = tiles(a["L1_ffn_w3"].T)
    d["w2"] = tiles(a["L1_ffn_w2"].T)
    d["wr"] = tiles(a["L1_ffn_wr"].T)
    return d


def kernel(**inputs):
    import concourse.bacc as bacc
    from concourse.bass_utils import run_bass_kernel_spmd

    nc = bacc.Bacc("TRN2", target_bir_lowering=False, num_devices=1)
    arrays, aps = {}, {}
    for name, a in laid_out(inputs).items():
        arrays[f"in_{name}"] = a
        aps[name] = nc.dram_tensor(f"in_{name}", a.shape, mybir.dt.from_np(a.dtype), kind="ExternalInput").ap()
    out = nc.dram_tensor("out_rows", (B, C, N), F32, kind="ExternalOutput").ap()
    program(nc, aps, out)
    r = run_bass_kernel_spmd(nc, [arrays], core_ids=[0])
    return r.results[0]["out_rows"]
```

```python
from contextlib import ExitStack

import concourse.bass as bass
from concourse import mybir

F32 = mybir.dt.float32
BF16 = mybir.dt.bfloat16
I32 = mybir.dt.int32
U32 = mybir.dt.uint32
ALU = mybir.AluOpType
ACT = mybir.ActivationFunctionType
AX = mybir.AxisListType

B, C, N = 8, 256, 512
CT = C // 128
TILES = B * CT
H, HD = 16, 16
MT = N // 128
QUAD = 4
LEAD = 7
PARTS = ((0, 0, 1, 0, 2, 1), (0, 1, 0, 2, 0, 1))
KST = 6 * HD + 3
EPS = 1e-5
MOMENT_OPS = 7
E_N, TOP, CAP, I_N = 64, 6, 128, 192
SI = 2 * I_N
SLOTS = E_N * CAP
KT = N // 128
AHEAD = 4
RING = 4
REST = I_N - 128
ZEROED = SLOTS // (16 * B)


class Chain:

    def __init__(self, engine, sem):
        self.engine, self.sem, self.base, self.n = engine, sem, 0, 0

    def __call__(self, instruction):
        self.n += 1
        instruction.then_inc(self.sem, 1)
        self.engine.wait_ge(self.sem, self.base + self.n)


def loading(nc, ctx, X, mem, x):
    x_in = [ctx.enter_context(nc.semaphore(f"x_in{n}")) for n in range(B // 2)]
    stats_chain = ctx.enter_context(nc.semaphore("stats_chain"))

    def on_sync(sp):
        for b in range(B):
            sp.dma_start(X[:, CT * b:CT * (b + 1), :], x[b].rearrange("(t p) n -> p t n", p=128))\
              .then_inc(x_in[b // 2], 16)

    def on_pool(pool):
        pool.memset(mem["zero"][:], 0.0).then_inc(mem["made"], 1)
        pool.memset(mem["ident"][:], 0.0).then_inc(mem["made"], 1)
        pool.wait_ge(mem["made"], 2)
        pool.affine_select(out=mem["ident"][:], in_=mem["ident"][:], compare_op=ALU.not_equal, fill=1.0, base=0,
                           pattern=[[-1, 128]], channel_multiplier=1).then_inc(mem["made"], 1)
        pool.wait_ge(mem["made"], 3)
        pool.tensor_copy(mem["ident_b"][:], mem["ident"][:]).then_inc(mem["made"], 1)

    def on_vector(dve, pairs):
        for n in pairs:
            dve.wait_ge(x_in[n], 32)
            for i in range(2 * CT * n, 2 * CT * (n + 1)):
                last = dve.bn_stats(mem["stats"][:, i, :], X[:, i, :])
        last.then_inc(stats_chain, 1)
        dve.wait_ge(stats_chain, 1 if pairs[0] == 0 else 2)

    return on_sync, on_pool, on_vector


class Moments:

    def __init__(self, nc, ctx, tag, mem, tiles, runs):
        def sb(name, shape):
            return ctx.enter_context(nc.sbuf_tensor(tag + name, shape, F32))

        self.nc, self.mem, self.tiles, self.first = nc, mem, tiles, mem["moment_runs"]
        mem["moment_runs"] += runs
        self.moment = sb("moment", [128, tiles, 2])
        self.var, self.root, self.err, self.rstd = (sb(n, [128, tiles]) for n in ("var", "root", "err", "rstd"))

    def mean_of(self, i):
        return self.moment[:, i, 0:1]

    def rstd_of(self, i):
        return self.rstd[:, i:i + 1] if isinstance(i, int) else self.rstd[:, bass.ds(i, 1)]

    def chain(self, dve, run, done):
        chain = Chain(dve, self.mem["moments_chain"])
        chain.base, chain.n = MOMENT_OPS * (self.first + run), done
        return chain

    def variances(self, dve, stats, run, some):
        chain = self.chain(dve, run, 0)
        for i in range(self.tiles)[some]:
            last = dve.bn_aggr(self.moment[:, i, :], stats[:, i, :])
        chain(last)
        chain(dve.tensor_scalar(self.var[:, some], self.moment[:, some, 1], EPS, None, ALU.add))

    def roots(self, act, run, some):
        act.wait_ge(self.mem["moments_chain"], MOMENT_OPS * (self.first + run) + 2)
        self.nc.scalar.activation(self.root[:, some], self.var[:, some], ACT.Sqrt).then_inc(self.mem["root_set"], 1)

    def reciprocals(self, dve, run, some):
        chain = self.chain(dve, run, 2)
        r, err, var = self.rstd[:, some], self.err[:, some], self.var[:, some]
        dve.wait_ge(self.mem["root_set"], self.first + run + 1)
        chain(dve.reciprocal(r, self.root[:, some]))
        chain(dve.tensor_tensor(err, r, r, ALU.mult))
        chain(dve.tensor_tensor(err, err, var, ALU.mult))
        chain(dve.tensor_scalar(err, err, -0.5, 1.5, ALU.mult, ALU.add))
        chain(dve.tensor_tensor(r, r, err, ALU.mult))
        assert chain.n == MOMENT_OPS, chain.n


def attention(nc, tag, dram, X, mem, scale, start=None):
    rotary = "enc" in dram
    combining = start is None
    ident_b = mem["ident_b"]
    with ExitStack() as ctx:
        def sb(name, shape, dt):
            return ctx.enter_context(nc.sbuf_tensor(tag + name, shape, dt))

        def pb(name, shape, dt):
            return ctx.enter_context(nc.psum_tensor(tag + name, shape, dt))

        def sem(name):
            return ctx.enter_context(nc.semaphore(tag + name))

        qst = [sb(f"qst{p}", [KST, H, N], BF16) for p in range(2)]
        kst = [sb(f"kst{p}", [KST, H, N], BF16) for p in range(2)]
        probs = [sb(f"probs{p}", [128, QUAD, N], F32) for p in range(2)]
        vz = [sb(f"vz{p}", [128, MT, H, 2 * HD], F32) for p in range(2)]
        wq, wk, wv, wo = (sb(n, [128, CT, C], F32) for n in ("wq", "wk", "wv", "wo"))
        biases = sb("biases", [128, 4, CT], F32)
        bo_all = sb("bo_all", [128, CT], F32)
        context = [sb(f"context{p}", [128, CT, N], F32) for p in range(2)]
        xn = sb("xn", [128, CT, N], F32)
        qf = [sb(f"qf{p}", [128, N], F32) for p in range(2)]
        parts = [sb(f"parts{p}", [128, 3, N], BF16) for p in range(2)]
        rest = sb("rest", [128, N], F32)
        if rotary:
            shuf = [sb(f"shuf{p}", [128, N], F32) for p in range(2)]
            cos_t, sin_t = sb("cos_t", [128, N], F32), sb("sin_t", [128, N], F32)
            sign = sb("sign", [128, 1], F32)
        mx = [sb(f"mx{p}", [128, 16], F32) for p in range(2)]
        mrest = sb("mrest", [128, 16], F32)
        msplit = [sb(f"msplit{p}", [128, 48], BF16) for p in range(2)]
        mrow = [sb(f"mrow{p}", [48, 128], BF16) for p in range(2)]
        u = [sb(f"u{p}", [128, N], F32) for p in range(2)]
        den = sb("den", [128, 64], F32)
        rden = sb("rden", [128, 64], F32)
        att = sb("att", [128, CT, N], F32)
        rfull = sb("rfull", [128, CT, N], F32)

        st = [pb(f"st{p}", [128, 2, N], F32) for p in range(2)]
        sc = [pb(f"sc{p}", [128, N], F32) for p in range(2)]
        o_ps = pb("o_ps", [128, N], F32)
        misc = pb("misc", [128, N], F32)

        scr = nc.dram_tensor(tag + "scr", [2, 2, 3, C, N], BF16, kind="Internal").ap()
        scr_u = nc.dram_tensor(tag + "scr_u", [2, H, 2 * HD, N], F32, kind="Internal").ap()
        scr_r = nc.dram_tensor(tag + "scr_r", [2, H, N], F32, kind="Internal").ap()

        weights_in = sem("weights_in")
        ones_set = sem("ones_set")
        ctx_in = [sem(f"ctx_in{p}") for p in range(2)]
        xn_set = sem("xn_set")
        bo_made, qk_made, v_made, o_made, t_made = (sem(n + "_made") for n in ("bo", "qk", "v", "o", "t"))
        bo_set = sem("bo_set")
        qf_set = sem("qf_set")
        shuf_set = sem("shuf_set")
        parts_set = sem("parts_set")
        parts_stored = [sem(f"parts_stored{p}") for p in range(2)]
        stacks_in = [sem(f"stacks_in{p}") for p in range(2)]
        vz_set = sem("vz_set")
        sc_set = sem("sc_set")
        max_set = sem("max_set")
        split_set = sem("split_set")
        mrow_set = sem("mrow_set")
        mrow_in = [sem(f"mrow_in{p}") for p in range(2)]
        st_set = sem("st_set")
        exp_set = sem("exp_set")
        pv_done = sem("pv_done")
        u_set = sem("u_set")
        u_stored = [sem(f"u_stored{p}") for p in range(2)]
        den_in = sem("den_in")
        num_in = sem("num_in")
        rden_set = sem("rden_set")
        rden_stored = sem("rden_stored")
        rfull_in = sem("rfull_in")
        att_set = sem("att_set")
        x_set = sem("x_set")
        dve_chain = sem("dve_chain")
        unit_chain = sem("unit_chain")
        max_chain = sem("max_chain")

        weight_dmas = 16 * (5 + (3 if rotary else 0))
        stack_dmas = 16 * 12
        QK = ["k0", "k1", "q0", "q1"]
        if combining:
            UNITS = [(2, "t"), (3, "k0"), (4, "v0"), (6, "t"), (8, "v1"), (9, "k1"), (10, "t"), (11, "o0"),
                     (12, "o1"), (13, "q0"), (14, "t"), (15, "q1")]
            TURNED, CUT, STORED, SCALED = (4, 10, 14), (5, 11, 14), (6, 12, 15), (9, 10)
        else:
            UNITS = [(2, "t"), (3, "k0"), (4, "v0"), (5, "v1"), (6, "t"), (7, "k1"), (10, "t"), (11, "q0"),
                     (12, "o0"), (13, "o1"), (14, "t"), (15, "q1")]
            TURNED, CUT, STORED, SCALED = (4, 8, 12), (5, 9, 13), (6, 10, 14), (10, 11)
        GATHERED = {0: (0, 0), 1: (0, 1), 6: (1, 0), 7: (1, 1)}
        COMBINED = {3: (0, 0), 4: (0, TOP // 2), 8: (1, 0), 9: (1, TOP // 2)}
        FIRST_UNITS = ([("bo", 0)] + [(n, 0) for n in ("k0", "k1", "v0", "v1", "q0", "q1")] +
                       [(n, 1) for n in QK[:2]] +
                       [("t", 0)] * combining + [("q0", 1)] + [("t", 0)] * (not combining) + [("q1", 1)])

        def has(kb, what, s=0):
            if what == "main":
                return kb < B
            if what == "qk":
                return kb + 2 < B
            if what == "v":
                return kb + 1 < B
            if what == "ahead":
                return 16 * kb + s + LEAD < 16 * B
            if what == "t":
                return (16 * kb + s + 2) // 4 < 4 * B
            return kb >= 1

        def unit_at(kb, b, s):
            name = dict(UNITS).get(s)
            if name is None or not has(kb, {"q": "qk", "k": "qk", "v": "v", "t": "t", "o": "out"}[name[0]], s):
                return None, None
            return name, {"q": b + 2, "k": b + 2, "v": b + 1, "o": b - 1, "t": 4 * b + (s + 2) // 4}[name[0]]

        def unit_before(kb, b, s):
            for at in range(s - 1, -1, -1):
                if unit_at(kb, b, at)[0]:
                    return unit_at(kb, b, at)
            if kb == 0:
                return FIRST_UNITS[-1]
            for at in range(15, -1, -1):
                if unit_at(kb - 1, b - 1, at)[0]:
                    return unit_at(kb - 1, b - 1, at)

        def over_batches(eng, body):
            for kb in range(2):
                body(kb, kb)
            with eng.Fori(1, (B - 2) // 2) as i:
                body(2, 2 * i)
                body(3, 2 * i + 1)
            for kb in range(B - 2, B + 1):
                body(kb, kb)

        def own(engine):
            engine.sem_inc(mem["passed"], 1)

        norm = Moments(nc, ctx, tag, mem, *((CT, B) if combining else (TILES, 2)))
        first, rest_of = (slice(0, CT), None) if combining else (slice(0, 2 * CT), slice(2 * CT, TILES))
        if combining:
            all_index, all_weight, expert_rows = mem["all_index"], mem["all_weight"], mem["expert_rows"]
            got = [sb(f"got{j}", [128, TOP // 2, N], F32) for j in range(2)]
            index = [sb(f"index{t}", [128, 8], I32) for t in range(CT)]
            fresh = sb("fresh", [128, CT, 6], F32)
            index_set = sem("index_set")
            got_in = [sem(f"got_in{j}") for j in range(2)]
            add_chain = sem("add_chain")
            fresh_set = sem("fresh_set")
        start_on_sync, start_on_pool, start_on_vector = start or 3 * (lambda *_: None,)
        block = ctx.enter_context(nc.Block())

        @block.sync
        def _(sp):
            for t, name in ((wq, "wq"), (wk, "wk"), (wv, "wv"), (wo, "wo"), (biases, "biases")):
                sp.dma_start(t[:], dram[name]).then_inc(weights_in, 16)
            if rotary:
                for t, n in ((cos_t, 0), (sin_t, 1)):
                    sp.dma_start(t[:], dram["enc"][n].unsqueeze(0).broadcast_to([128 // HD, HD, N]))\
                      .then_inc(weights_in, 16)
                sp.dma_start(sign[:], dram["sign"]).then_inc(weights_in, 16)

            def load_context(b, p):
                sp.dma_start(context[p][:], dram["ctx"][b].rearrange("(t p) n -> p t n", p=128))\
                  .then_inc(ctx_in[p], 16)

            def store_parts(b, p, unit):
                j = QK.index(unit)
                sp.wait_ge(parts_set, 4 * b + j + 1)
                sp.dma_start(scr[p, 1 - j // 2, :, 128 * (j % 2):128 * (j % 2 + 1), :].rearrange("s c n -> c s n"),
                             parts[j % 2][:]).then_inc(parts_stored[j % 2], 16)

            def load_stacks(b, p, then_stored=()):
                for which, dst in ((1, kst[p]), (0, qst[p])):
                    for j in range(2):
                        sp.wait_ge(parts_stored[j], 32 * b + 32 - 16 * which)
                        own(sp)
                    for r, part in enumerate(PARTS[which]):
                        sp.dma_start(dst[HD * r:HD * (r + 1), :, :],
                                     scr[p, which, part].rearrange("(h d) n -> d h n", d=HD))\
                          .then_inc(stacks_in[p], 16)
                    for unit in then_stored if which == 1 else ():
                        store_parts(b, p, unit)

            def store_row_max(b, p, quad):
                sp.wait_ge(mrow_set, 4 * b + quad + 1)
                sp.dma_start(qst[p][KST - 3:KST, QUAD * quad:QUAD * (quad + 1), :]
                             .rearrange("s h (t n) -> s (h t) n", n=128),
                             mrow[quad % 2][:]).then_inc(mrow_in[quad % 2], 16)

            def store_values(b, p, quad):
                sp.wait_ge(u_set, 4 * b + quad + 1)
                sp.dma_start(scr_u[p, QUAD * quad:QUAD * (quad + 1)].rearrange("h r n -> (h r) n"),
                             u[quad % 2][:]).then_inc(u_stored[quad % 2], 16)

            load_context(0, 0)
            start_on_sync(sp)
            load_context(1, 1)
            for unit in QK[:2]:
                store_parts(0, 0, unit)
            load_stacks(0, 0, QK[2:])
            for unit in QK[:2]:
                store_parts(1, 1, unit)
            store_row_max(0, 0, 0)
            store_parts(1, 1, QK[2])

            def body(kb, b):
                p = kb % 2
                for s in range(16):
                    if s == 0 and has(kb, "qk"):
                        sp.wait_ge(vz_set, 2 * (b + 1))
                        load_context(b + 2, p)
                    if s == 1 and has(kb, "out"):
                        store_values(b - 1, 1 - p, 3)
                    if s in (2, 6, 10, 14) and has(kb, "t", s):
                        store_row_max(*((b, p, (s + 2) // 4) if s < 14 else (b + 1, 1 - p, 0)))
                    if s == 3 and has(kb, "out"):
                        for j in range(2):
                            sp.wait_ge(u_stored[j], 32 * b)
                        if kb >= 2:
                            own(sp)
                            sp.wait_ge(rden_set, b - 1)
                            own(sp)
                            sp.wait_ge(x_set, 2 * (b - 1))
                        own(sp)
                        sp.dma_start(den[:], scr_u[1 - p, :, HD, :].rearrange("h (c f) -> h c f", f=64))\
                          .then_inc(den_in, 16)
                        for t in range(CT):
                            sp.dma_start(att[:, t, :], scr_u[1 - p, 8 * t:8 * (t + 1), 0:HD, :]).then_inc(num_in, 16)
                    if s == 2 and has(kb, "v"):
                        store_parts(b + 1, 1 - p, QK[3])
                    if s == 3 and has(kb, "v"):
                        if kb >= 1:
                            sp.wait_ge(st_set, 32 * b)
                            own(sp)
                        load_stacks(b + 1, 1 - p)
                    if s == 7 and has(kb, "out"):
                        sp.wait_ge(rden_set, b)
                        own(sp)
                        if kb >= 2:
                            sp.wait_ge(rfull_in, 32 * (b - 1))
                            own(sp)
                        sp.dma_start(scr_r[1 - p].rearrange("h (c f) -> h c f", f=64), rden[:])\
                          .then_inc(rden_stored, 16)
                        sp.wait_ge(rden_stored, 16 * b)
                        own(sp)
                        for t in range(CT):
                            sp.dma_start(rfull[:, t, :], scr_r[1 - p, 8 * t:8 * (t + 1)].unsqueeze(1)
                                         .broadcast_to([8, HD, N])).then_inc(rfull_in, 16)
                    if s in (5, 9, 13) and has(kb, "main"):
                        if s == 5 and kb >= 1:
                            sp.wait_ge(den_in, 16 * b)
                            own(sp)
                            sp.wait_ge(num_in, 32 * b)
                            own(sp)
                        store_values(b, p, (s - 1) // 4 - 1)
                    if has(kb, "qk"):
                        if s == 6:
                            sp.wait_ge(stacks_in[p], stack_dmas // 2 * (b - p) + stack_dmas)
                            own(sp)
                        if s in STORED:
                            store_parts(b + 2, p, QK[STORED.index(s)])

            over_batches(sp, body)

        @block.tensor
        def _(pe):
            pe.wait_ge(mem["made"], 4)
            evacuated = {"bo": lambda b: (bo_set, 1), "t": lambda q: (mrow_set, q + 1),
                         "v": lambda b, j: (vz_set, 2 * b + j + 1), "o": lambda b, j: (x_set, 2 * b + j + 1),
                         "k": lambda b, j: (qf_set, 4 * b + j + 1), "q": lambda b, j: (qf_set, 4 * b + j + 3)}

            def bank_free(name, b):
                if name in ("bo", "t"):
                    pe.wait_ge(*evacuated[name](b))
                else:
                    pe.wait_ge(*evacuated[name[0]](b, int(name[1])))

            def unit(name, b, p):
                if name == "bo":
                    for t in range(CT):
                        for c in range(CT):
                            mm = pe.matmul(misc[:, t:t + 1], wo[:, c, 128 * t:128 * (t + 1)], biases[:, 2, c:c + 1],
                                           start=(c == 0), stop=(c == CT - 1))
                    mm.then_inc(bo_made, 1)
                elif name[0] in "qk":
                    if name[0] == "q":
                        pe.wait_ge(xn_set, b + 1)
                    else:
                        pe.wait_ge(ctx_in[p], 8 * (b - p) + 16)
                    w, src = (wq, xn) if name[0] == "q" else (wk, context[p])
                    t = int(name[1])
                    for c in range(CT):
                        mm = pe.matmul(misc[:], w[:, c, 128 * t:128 * (t + 1)], src[:, c, :],
                                       start=(c == 0), stop=(c == CT - 1))
                    mm.then_inc(qk_made, 1)
                elif name[0] == "v":
                    pe.wait_ge(ctx_in[p], 8 * (b - p) + 16)
                    for j in range(2):
                        mt = 2 * int(name[1]) + j
                        for c in range(CT):
                            mm = pe.matmul(misc[:, C * j:C * (j + 1)], context[p][:, c, 128 * mt:128 * (mt + 1)],
                                           wv[:, c, :], start=(c == 0), stop=(c == CT - 1))
                    mm.then_inc(v_made, 1)
                elif name[0] == "o":
                    pe.wait_ge(att_set, 2 * (b + 1))
                    t = int(name[1])
                    for c in range(CT):
                        mm = pe.matmul(misc[:], wo[:, c, 128 * t:128 * (t + 1)], att[:, c, :],
                                       start=(c == 0), stop=(c == CT - 1))
                    mm.then_inc(o_made, 1)

            def turn_max(q, quad):
                pe.wait_ge(split_set, q + 1)
                pe.matmul(misc[0:48, 0:128], msplit[quad % 2][:], ident_b[:], start=True, stop=True).then_inc(t_made, 1)

            def plain_scores(head, p, h, nt):
                pe.wait_ge(max_set, 4 * head + nt + 1)
                pe.matmul(sc[nt % 2][:], qst[p][0:KST - 3, h, 128 * nt:128 * (nt + 1)], kst[p][0:KST - 3, h, :],
                          start=True, stop=True).then_inc(sc_set, 1)

            def weigh(g, b, kb, p, quad, mt):
                pe.wait_ge(exp_set, 2 * g + 4)
                if mt == 0:
                    pe.wait_ge(vz_set, 2 * (b + 1))
                    if kb > 0 or quad > 0:
                        pe.wait_ge(u_set, 4 * b + quad)
                for j in range(QUAD):
                    mm = pe.matmul(o_ps[32 * j:32 * (j + 1), :], vz[p][:, mt, QUAD * quad + j, :],
                                   probs[mt % 2][:, j, :], start=(mt == 0), stop=(mt == MT - 1))
                mm.then_inc(pv_done, 1)

            pe.wait_ge(weights_in, weight_dmas)
            for n, (name, b) in enumerate(FIRST_UNITS):
                if name == "t":
                    pe.wait_ge(stacks_in[0], stack_dmas)
                    for head in range(LEAD):
                        for nt in range(MT):
                            plain_scores(head, 0, head, nt)
                bank_free(*FIRST_UNITS[n - 1]) if n else None
                if name == "t":
                    turn_max(0, 0)
                else:
                    unit(name, b, b)

            def body(kb, b):
                p = kb % 2
                for s in range(16):
                    quad, mt = s // 4, s % 4
                    g = 16 * b + s
                    ahead = s + LEAD

                    def scores_ahead(nt):
                        if has(kb, "ahead", s):
                            plain_scores(16 * b + ahead, p if ahead < 16 else 1 - p, ahead % 16, nt)

                    if has(kb, "main"):
                        if mt == 0:
                            pe.wait_ge(mrow_in[quad % 2], 16 * (2 * b + quad // 2 + 1))
                        for j in range(QUAD):
                            h = QUAD * quad + j
                            if j % 2 == 0:
                                pe.wait_ge(exp_set, 2 * g + j // 2 + 1)
                            mm = pe.matmul(st[j // 2][:, j % 2, :], kst[p][:, h, 128 * mt:128 * (mt + 1)],
                                           qst[p][:, h, :], start=True, stop=True)
                            if j == 1:
                                mm.then_inc(st_set, 1)
                                if ahead == 16 and has(kb, "ahead", s):
                                    pe.wait_ge(stacks_in[1 - p], stack_dmas // 2 * (b + 1 - (1 - p)) + stack_dmas)
                                scores_ahead(0)
                            if j == 3:
                                mm.then_inc(st_set, 1)
                                scores_ahead(1)
                    if s > 0 and has(kb, "main"):
                        weigh(g - 1, b, kb, p, (s - 1) // 4, (s - 1) % 4)
                    if s == 0 and kb > 0:
                        weigh(g - 1, b - 1, kb - 1, 1 - p, 3, 3)
                    scores_ahead(2)
                    name, ub = unit_at(kb, b, s)
                    if name:
                        bank_free(*unit_before(kb, b, s))
                        if name == "t":
                            turn_max(ub, (s + 2) // 4 % 4)
                        else:
                            unit(name, ub, p if name in QK else 1 - p)
                    scores_ahead(3)

            pe.wait_ge(ones_set, 4)
            over_batches(pe, body)

        @block.scalar
        def _(act):
            act.sem_inc(exp_set, 2)
            act.wait_ge(weights_in, weight_dmas)

            def project_out(name, b, kb):
                j = QK.index(name)
                act.wait_ge(qk_made, 4 * b + j + 1)
                if kb > 0 or j >= 2:
                    act.wait_ge(parts_set, 4 * b + j - 1)
                nc.scalar.activation(qf[j % 2][:], misc[:], ACT.Identity,
                                     bias=biases[:, 1 - j // 2, j % 2:j % 2 + 1]).then_inc(qf_set, 1)

            def values_out(name, b, kb, p):
                half = int(name[1])
                act.wait_ge(v_made, 2 * b + half + 1)
                if kb >= 2:
                    act.wait_ge(pv_done, 16 * (b - 1))
                nc.scalar.copy(vz[p][:, 2 * half:2 * half + 2, :, 0:HD],
                               misc[:].rearrange("p (t h d) -> p t h d", t=2, d=HD)).then_inc(vz_set, 1)

            def max_rows(q, quad, first):
                act.wait_ge(t_made, q + 1)
                if not first:
                    act.wait_ge(mrow_in[quad % 2], 8 * (q - quad % 2))
                nc.scalar.copy(mrow[quad % 2][:], misc[0:48, 0:128]).then_inc(mrow_set, 1)

            for name, b in FIRST_UNITS:
                if name == "t":
                    max_rows(0, 0, True)
                if name == "q0" and (combining or b == 0):
                    norm.roots(act, b, first)
                if name in QK:
                    project_out(name, b, b)
                elif name[0] == "v":
                    values_out(name, b, b, b)
            if not combining:
                norm.roots(act, 1, rest_of)

            def body(kb, b):
                p = kb % 2
                for s in range(16):
                    quad, mt = s // 4, s % 4
                    g = 16 * b + s
                    if has(kb, "main"):
                        for half in range(2):
                            act.wait_ge(st_set, 2 * g + half + 1)
                            if half == 0 and (kb > 0 or s >= 2):
                                act.wait_ge(pv_done, g - 1)
                            nc.scalar.activation(probs[mt % 2][:, 2 * half:2 * half + 2, :], st[half][:], ACT.Exp,
                                                 scale=scale).then_inc(exp_set, 1)
                    if mt == 0 and (kb > 0 or s > 0) and (has(kb, "main") or s == 0):
                        before = quad - 1
                        act.wait_ge(pv_done, 16 * b + 4 * quad)
                        if kb > 0 or quad > 2:
                            act.wait_ge(u_stored[before % 2], 16 * (2 * b + (before - before % 2) // 2))
                        nc.scalar.copy(u[before % 2][:], o_ps[:]).then_inc(u_set, 1)
                    if not combining and has(kb, "main") and mt == 3:
                        act.dma_start(mem["slot_rows"][bass.ds(16 * ZEROED * b + 4 * ZEROED * quad, 4 * ZEROED), :]
                                      .rearrange("(c j) n -> c j n", c=128), mem["zero"][:].unsqueeze(1)
                                      .broadcast_to([128, 4 * ZEROED // 128, N])).then_inc(mem["zeroed"], 16)
                    if combining and s == 10 and has(kb, "qk"):
                        norm.roots(act, b + 2, first)
                    name, ub = unit_at(kb, b, s)
                    if name in QK:
                        project_out(name, ub, kb + 2)
                    elif name and name[0] == "v":
                        values_out(name, ub, kb + 1, 1 - p)
                    elif name == "t":
                        max_rows(ub, (s + 2) // 4, kb == 0 and s == 2)

            if not combining:
                act.wait_ge(mem["made"], 4)
                act.dma_start(mem["expert_rows"][SLOTS:SLOTS + 1, :], mem["zero"][0:1, :])\
                   .then_inc(mem["zeroed"], 16)
            over_batches(act, body)

        @block.vector
        def _(dve):
            chained = 0

            def chain(instruction):
                nonlocal chained
                chained += 1
                instruction.then_inc(dve_chain, 1)
                dve.wait_ge(dve_chain, chained)

            dve.sem_inc(max_set, 2)
            dve.wait_ge(weights_in, weight_dmas)
            if rotary:
                chain(dve.tensor_scalar(sin_t[:], sin_t[:], sign[:], None, ALU.mult))
            dve.wait_ge(bo_made, 1)
            dve.tensor_tensor(bo_all[:], misc[:, 0:CT], biases[:, 3, :], ALU.add).then_inc(bo_set, 1)

            def normalise(b, kb):
                if kb > 0:
                    dve.wait_ge(qf_set, 4 * b)
                for t in range(CT):
                    i, j = CT * b + t, t if combining else CT * b + t
                    normal = dve.tensor_scalar(xn[:, t, :], X[:, i, :], norm.mean_of(j), norm.rstd_of(j),
                                               ALU.subtract, ALU.mult)
                normal.then_inc(xn_set, 1)

            def combine(b, t, choice):
                i, j, k = CT * b + t, choice // (TOP // 2), choice % (TOP // 2)
                if k == 0:
                    dve.wait_ge(got_in[j], 16 * (TOP // 2) * (i + 1))
                if not isinstance(b, int) or choice or i:
                    dve.wait_ge(add_chain, TOP * i + choice)
                dve.scalar_tensor_tensor(X[:, i, :], got[j][:, k, :], all_weight[:, i, choice:choice + 1],
                                         X[:, i, :], ALU.mult, ALU.add).then_inc(add_chain, 1)
                if choice == TOP - 1:
                    dve.wait_ge(add_chain, TOP * (i + 1))
                    own(dve)
                    dve.bn_stats(fresh[:, t, :], X[:, i, :]).then_inc(fresh_set, 1)

            def variances(b):
                dve.wait_ge(fresh_set, CT * (b + 1))
                own(dve)
                norm.variances(dve, fresh, b, first)

            def shuffle_unit(name, b, kb):
                j = QK.index(name)
                if rotary:
                    dve.wait_ge(qf_set, 4 * b + j + 1)
                    own(dve)
                    dve.stream_shuffle(shuf[j % 2][:], qf[j % 2][:], [n ^ 1 for n in range(32)]).then_inc(shuf_set, 1)

            def maxima(head, q, quad, mt, first, between=None):
                if mt == 0 and not first:
                    dve.wait_ge(split_set, q - 1)
                for nt in range(MT):
                    dve.wait_ge(sc_set, 4 * head + nt + 1)
                    dve.tensor_reduce(mx[quad % 2][:, 4 * mt + nt:4 * mt + nt + 1], sc[nt % 2][:], AX.X, ALU.max,
                                      negate=True).then_inc(max_set, 1)
                    if between and nt > 0:
                        combine(between[0], between[1], between[2] + nt - 1)

            for j, name in enumerate(QK):
                if combining and j < CT:
                    for choice in range(TOP):
                        combine(0, j, choice)
                if j == (1 if combining else 2):
                    if combining:
                        variances(0)
                    else:
                        start_on_vector(dve, [0])
                        norm.variances(dve, mem["stats"], 0, first)
                    norm.reciprocals(dve, 0, first)
                    normalise(0, 0)
                shuffle_unit(name, 0, 0)
                dve.wait_ge(qf_set, j + 1)
                if j >= 2:
                    dve.wait_ge(parts_stored[j % 2], 16)
                q = qf[j % 2][:]
                hi, mid, lo = (parts[j % 2][:, n, :] for n in range(3))
                if rotary:
                    dve.wait_ge(shuf_set, j + 1)
                    chain(dve.tensor_tensor(shuf[j % 2][:], shuf[j % 2][:], sin_t[:], ALU.mult))
                    chain(dve.tensor_tensor(q, q, cos_t[:], ALU.mult))
                    chain(dve.tensor_tensor(q, q, shuf[j % 2][:], ALU.add))
                chain(dve.tensor_copy(hi, q))
                chain(dve.tensor_tensor(rest[:], q, hi, ALU.subtract))
                chain(dve.tensor_copy(mid, rest[:]))
                dve.tensor_tensor(lo, rest[:], mid, ALU.subtract).then_inc(parts_set, 1)
            for name in QK[:2]:
                shuffle_unit(name, 1, 1)
            if not combining:
                normalise(1, 1)
                start_on_vector(dve, range(1, B // 2))
                norm.variances(dve, mem["stats"], 1, rest_of)
            for head in range(LEAD):
                if head == 3 and not combining:
                    shuffle_unit(QK[2], 1, 1)
                maxima(head, head // 4, head // 4, head % 4, True,
                       (1, head // QUAD, TOP // 2 * (head % QUAD)) if combining and head % QUAD < 2 else None)
            if combining:
                variances(1)
                norm.reciprocals(dve, 1, first)
                normalise(1, 1)
                shuffle_unit(QK[2], 1, 1)
            shuffle_unit(QK[3], 1, 1)
            if not combining:
                norm.reciprocals(dve, 1, rest_of)

            def body(kb, b):
                p = kb % 2
                for s in range(16):
                    if has(kb, "ahead", s):
                        ahead = s + LEAD
                        maxima(16 * b + ahead, 4 * b + ahead // 4, ahead // 4, ahead % 4, kb == 0 and ahead < 8,
                               (b + 2, *COMBINED[s]) if combining and has(kb, "qk") and s in COMBINED else None)
                    if s == 6 and has(kb, "out"):
                        dve.wait_ge(den_in, 16 * b)
                        if kb >= 2:
                            dve.wait_ge(rden_stored, 16 * (b - 1))
                        dve.reciprocal(rden[:], den[:]).then_inc(rden_set, 1)
                    if combining and has(kb, "qk"):
                        if s == 10:
                            variances(b + 2)
                        if s == 11:
                            norm.reciprocals(dve, b + 2, first)
                    if s == (12 if combining else 9) and has(kb, "qk"):
                        normalise(b + 2, kb + 2)
                    name, ub = unit_at(kb, b, s)
                    if name in QK:
                        shuffle_unit(name, ub, kb + 2)
                    elif name and name[0] == "o":
                        t = int(name[1])
                        dve.wait_ge(o_made, 2 * ub + t + 1)
                        tile = CT * ub + t
                        dve.scalar_tensor_tensor(X[:, tile, :], misc[:], bo_all[:, t:t + 1], X[:, tile, :],
                                                 ALU.add, ALU.add).then_inc(x_set, 1)
                    if s in (14, 15) and has(kb, "out"):
                        tile = CT * (b - 1) + s - 14
                        dve.wait_ge(x_set, tile + 1)
                        dve.bn_stats(mem["stats"][:, tile, :], X[:, tile, :])

            over_batches(dve, body)

        @block.gpsimd
        def _(pool):
            chained = 6 if rotary else 3

            def rotate(name, b):
                j = QK.index(name)
                m = 4 * (b - 1) + j
                pool.wait_ge(parts_set, 4 * b + j)
                if rotary:
                    pool.wait_ge(shuf_set, 4 * b + j + 1)
                    q, sh = qf[j % 2][:], shuf[j % 2][:]
                    pool.tensor_tensor(sh, sh, sin_t[:], ALU.mult).then_inc(unit_chain, 1)
                    pool.tensor_tensor(q, q, cos_t[:], ALU.mult).then_inc(unit_chain, 1)
                    pool.wait_ge(unit_chain, chained * m + 2)
                    pool.tensor_tensor(q, q, sh, ALU.add).then_inc(unit_chain, 1)

            def split(name, b):
                j = QK.index(name)
                done = chained * (4 * (b - 1) + j) + chained - 3
                pool.wait_ge(qf_set, 4 * b + j + 1)
                if rotary:
                    pool.wait_ge(unit_chain, done)
                pool.wait_ge(parts_stored[j % 2], 16 * (2 * b + j // 2))
                q = qf[j % 2][:]
                hi, mid, lo = (parts[j % 2][:, n, :] for n in range(3))
                own(pool)
                pool.tensor_copy(hi, q).then_inc(unit_chain, 1)
                pool.wait_ge(unit_chain, done + 1)
                pool.tensor_tensor(rest[:], q, hi, ALU.subtract).then_inc(unit_chain, 1)
                pool.wait_ge(unit_chain, done + 2)
                own(pool)
                pool.tensor_copy(mid, rest[:]).then_inc(unit_chain, 1)
                pool.wait_ge(unit_chain, done + 3)
                pool.tensor_tensor(lo, rest[:], mid, ALU.subtract).then_inc(parts_set, 1)

            def split_max(q, quad, first, very_first):
                pool.wait_ge(max_set, 16 * (q + 1) + 2)
                if not first:
                    pool.wait_ge(mrow_set, q - 1)
                if not very_first:
                    pool.wait_ge(split_set, q)
                m, ms = mx[quad % 2][:], msplit[quad % 2]
                own(pool)
                pool.tensor_copy(ms[:, 0:16], m).then_inc(max_chain, 1)
                pool.wait_ge(max_chain, 3 * q + 1)
                pool.tensor_tensor(mrest[:], m, ms[:, 0:16], ALU.subtract).then_inc(max_chain, 1)
                pool.wait_ge(max_chain, 3 * q + 2)
                own(pool)
                pool.tensor_copy(ms[:, 16:32], mrest[:]).then_inc(max_chain, 1)
                pool.wait_ge(max_chain, 3 * q + 3)
                pool.tensor_tensor(ms[:, 32:48], mrest[:], ms[:, 16:32], ALU.subtract).then_inc(split_set, 1)

            start_on_pool(pool)
            def gather(b, t, j, first):
                i = CT * b + t
                if not first:
                    pool.wait_ge(add_chain, TOP * (i - 1) + TOP // 2 * (j + 1))
                if j == 0:
                    pool.tensor_copy(index[t][:], all_index[:, i, :]).then_inc(index_set, 1)
                    pool.wait_ge(index_set, i + 1)
                own(pool)
                for k in range(TOP // 2):
                    choice = TOP // 2 * j + k
                    pool.indirect_dma_start(out=got[j][:, k, :], out_offset=None, in_=expert_rows,
                                            in_offset=bass.IndirectOffsetOnAxis(
                                                index[t][:, choice:choice + 1].bitcast(U32), 0))\
                        .then_inc(got_in[j], 16)

            if combining:
                for t in range(CT):
                    for j in range(2):
                        gather(0, t, j, t == 0)
            for p in range(2):
                pool.memset(vz[p][:, :, :, HD:2 * HD], 1.0).then_inc(ones_set, 1)
                pool.wait_ge(ones_set, 2 * p + 1)
                pool.memset(kst[p][KST - 3:KST, :, :], 1.0).then_inc(ones_set, 1)
                pool.wait_ge(ones_set, 2 * p + 2)
            pool.wait_ge(weights_in, weight_dmas)
            for t, name in enumerate(QK[:2]):
                if combining:
                    for j in range(2):
                        gather(1, t, j, False)
                rotate(name, 1)
                split(name, 1)
            split_max(0, 0, True, True)
            rotate(QK[2], 1)
            split(QK[2], 1)

            def body(kb, b):
                for s in range(16):
                    if s in (1, 5, 9, 13) and has(kb, "t", s + 1):
                        quad = (s + 3) // 4
                        split_max(4 * b + quad, quad, kb == 0 and quad < 2, False)
                    if combining and has(kb, "qk") and s in GATHERED:
                        gather(b + 2, *GATHERED[s], False)
                    if s == 0 and has(kb, "v"):
                        rotate(QK[3], b + 1)
                    if s == 1 and has(kb, "v"):
                        split(QK[3], b + 1)
                    if s in SCALED and has(kb, "out"):
                        t = SCALED.index(s)
                        pool.wait_ge(num_in, 32 * b)
                        pool.wait_ge(rfull_in, 32 * b)
                        pool.tensor_tensor(att[:, t, :], att[:, t, :], rfull[:, t, :], ALU.mult).then_inc(att_set, 1)
                    if has(kb, "qk"):
                        for n, (turn, cut) in enumerate(zip(TURNED, CUT)):
                            if s == turn:
                                rotate(QK[n], b + 2)
                            if s == cut:
                                split(QK[n], b + 2)

            over_batches(pool, body)
def mixture(nc, d, X, mem):
    ident, all_index, all_weight = mem["ident"], mem["all_index"], mem["all_weight"]
    slot_rows, expert_rows = mem["slot_rows"], mem["expert_rows"]
    with ExitStack() as ctx:
        def sb(name, shape, dt):
            return ctx.enter_context(nc.sbuf_tensor("m0" + name, shape, dt))

        def pb(name, shape, dt):
            return ctx.enter_context(nc.psum_tensor("m0" + name, shape, dt))

        def sem(name):
            return ctx.enter_context(nc.semaphore("m0" + name))

        gate_w = sb("gate_w", [128, KT, E_N], F32)
        sg_w = sb("sg_w", [128, KT, SI], F32)
        su_w = sb("su_w", [128, KT, SI], F32)
        sd_w = sb("sd_w", [128, SI // 128, N], F32)
        w1 = [sb(f"w1_{r}", [128, KT, 2 * I_N], F32) for r in range(RING)]
        w2 = [sb(f"w2_{r}", [128, 2, N], F32) for r in range(RING)]
        xl = [sb(f"xl{n}", [128, N], F32) for n in range(AHEAD)]
        xT = [sb(f"xT{p}", [128, KT, 128], F32) for p in range(2)]
        silu = sb("silu", [128, SI], F32)
        hid = [sb(f"hid{p}", [128, SI], F32) for p in range(2)]
        before = sb("before", [128, 128], BF16)
        ones = sb("ones", [128, 128], BF16)
        first_slot = sb("first_slot", [128, E_N], F32)
        first_slot_i = sb("first_slot_i", [128, E_N], I32)
        nmax = sb("nmax", [128, 1], F32)
        total = sb("total", [128, 1], F32)
        rtotal = sb("rtotal", [128, 1], F32)
        ex = sb("ex", [128, E_N], F32)
        pp = sb("pp", [128, E_N + 8], F32)
        left = sb("left", [128, E_N + 8], F32)
        best = sb("best", [128, 8], F32)
        chosen = [sb(f"chosen{p}", [128, E_N], BF16) for p in range(2)]
        so_far = [sb(f"so_far{p}", [128, E_N], BF16) for p in range(2)]
        kept = sb("kept", [128, E_N], F32)
        weight = sb("weight", [128, E_N], F32)
        slot = sb("slot", [128, E_N], F32)
        slots8 = sb("slots8", [128, 8], F32)
        dropped = sb("dropped", [128, 8], F32)
        matches = sb("matches", [128, TOP, E_N], F32)
        index = [sb(f"index{n}", [128, 8], I32) for n in range(AHEAD)]
        gx = [sb(f"gx{r}", [128, N], F32) for r in range(RING)]
        gxT = [sb(f"gxT{p}", [128, KT, 128], F32) for p in range(2)]
        sg = sb("sg", [128, 2, 128], F32)
        hx = [sb(f"hx{p}", [128, 2, 128], F32) for p in range(2)]
        eo = [sb(f"eo{p}", [128, N], F32) for p in range(2)]

        tp = [pb(f"tp{p}", [128, KT, 128], F32) for p in range(2)]
        wide = [pb(f"wide{p}", [128, N], F32) for p in range(2)]
        logits, place = (pb(n, [128, N], F32)[:, 0:E_N] for n in ("logits", "place"))
        down = [pb(f"down{p}", [128, N], F32) for p in range(2)]

        weights_in = [sem(f"weights_in{n}") for n in range(2)]
        experts_in = [sem(f"experts_in{r}") for r in range(RING)]
        consts_set = sem("consts_set")
        xl_set, turned, xT_set = sem("xl_set"), sem("turned"), sem("xT_set")
        logits_made, nmax_set, ex_set = sem("logits_made"), sem("nmax_set"), sem("ex_set")
        wide_made, silu_set, hid_set = sem("wide_made"), sem("silu_set"), sem("hid_set")
        chosen_set, place_made, place_read = sem("chosen_set"), sem("place_made"), sem("place_read")
        down_made, added = sem("down_made"), sem("added")
        index_set = sem("index_set")
        scattered = [sem(f"scattered{n}") for n in range(AHEAD)]
        route_chain = sem("route_chain")
        gx_in = [sem(f"gx_in{r}") for r in range(RING)]
        gx_turned, gxT_set = sem("gx_turned"), sem("gxT_set")
        both_made, sg_set, hx_set = sem("both_made"), sem("sg_set"), sem("hx_set")
        out_made, eo_set = sem("out_made"), sem("eo_set")
        eo_stored = [sem(f"eo_stored{p}") for p in range(2)]

        def own(engine):
            engine.sem_inc(mem["passed"], 1)

        norm = Moments(nc, ctx, "m0", mem, TILES, 1)
        ROUTE_OPS = 22
        def over_tiles(eng, tile):
            for t in range(AHEAD):
                tile(t, t)
            with eng.Fori(1, TILES // AHEAD - 1) as i:
                for n in range(AHEAD):
                    tile(AHEAD + n, AHEAD * i + n)
            for t in range(TILES - AHEAD, TILES):
                tile(t, t)

        block = ctx.enter_context(nc.Block())

        @block.sync
        def _(sp):
            for n, t, name in ((0, gate_w, "gate_w"), (0, sg_w, "shared_gate"), (1, su_w, "shared_up"),
                               (1, sd_w, "shared_down")):
                sp.dma_start(t[:], d[name]).then_inc(weights_in[n], 16)

            def load_expert(e, r):
                sp.dma_start(w1[r][:], d["gate_up"][e].rearrange("(p t) i -> p t i", t=KT)).then_inc(experts_in[r], 16)
                sp.dma_start(w2[r][:, 0, :], d["down"][e][0:128, :]).then_inc(experts_in[r], 16)
                sp.dma_start(w2[r][128 - REST:128, 1, :], d["down"][e][128:I_N, :]).then_inc(experts_in[r], 16)

            def load_tokens(e, r):
                sp.dma_start(gx[r][:], slot_rows[CAP * e:CAP * (e + 1), :] if isinstance(e, int)
                             else slot_rows[bass.ds(CAP * e, CAP), :]).then_inc(gx_in[r], 16)

            def store_rows_of(e, p):
                sp.wait_ge(eo_set, e + 1)
                own(sp)
                sp.dma_start(expert_rows[CAP * e:CAP * (e + 1), :] if isinstance(e, int)
                             else expert_rows[bass.ds(CAP * e, CAP), :], eo[p][:]).then_inc(eo_stored[p], 16)

            for r in range(RING):
                load_expert(r, r)
            for n in range(AHEAD):
                sp.wait_ge(scattered[n], 16 * TOP * TILES // AHEAD)
            for r in range(RING):
                load_tokens(r, r)

            def expert(e, ke, r, ahead):
                if ahead:
                    sp.wait_ge(gx_turned, e + 1)
                    own(sp)
                    load_tokens(e + RING, r)
                if ke > 0:
                    store_rows_of(e - 1, (r - 1) % 2)
                    if ahead or r == 0:
                        load_expert(e - 1 + RING, (r - 1) % RING)

            for r in range(RING):
                expert(r, r, r, True)
            with sp.Fori(1, E_N // RING - 1) as i:
                for r in range(RING):
                    expert(RING * i + r, RING + r, r, True)
            for r in range(RING):
                expert(E_N - RING + r, E_N - RING + r, r, False)
            store_rows_of(E_N - 1, 1)
            for p in range(2):
                sp.wait_ge(eo_stored[p], 16 * E_N // 2)

        @block.tensor
        def _(pe):
            def turn(t, kt, first):
                p = kt % 2
                pe.wait_ge(xl_set, t + 1)
                if not first:
                    pe.wait_ge(xT_set, t - 1)
                for k in range(KT):
                    mm = pe.transpose(tp[p][:, k, :], xl[kt % AHEAD][:, 128 * k:128 * (k + 1)], ident[:])
                mm.then_inc(turned, 1)

            def shared_down(t, kt, p):
                pe.wait_ge(hid_set, t + 1)
                if kt >= 1:
                    pe.wait_ge(added, t)
                for k in range(SI // 128):
                    mm = pe.matmul(down[p][:], hid[p][:, 128 * k:128 * (k + 1)], sd_w[:, k, :],
                                   start=(k == 0), stop=(k == SI // 128 - 1))
                mm.then_inc(down_made, 1)

            def tile(kt, t):
                p = kt % 2
                pe.wait_ge(xT_set, t + 1)
                if kt > 0:
                    pe.wait_ge(ex_set, t)
                for k in range(KT):
                    mm = pe.matmul(logits, xT[p][:, k, :], gate_w[:, k, :], start=(k == 0), stop=(k == KT - 1))
                mm.then_inc(logits_made, 1)
                if kt > 0:
                    pe.wait_ge(hid_set, t)
                for n, w in enumerate((sg_w, su_w)):
                    if kt == 0 and n == 1:
                        pe.wait_ge(weights_in[1], 32)
                    for m in range(SI // 128):
                        for k in range(KT):
                            mm = pe.matmul(wide[n][:, 128 * m:128 * (m + 1)], w[:, k, 128 * m:128 * (m + 1)],
                                           xT[p][:, k, :], start=(k == 0), stop=(k == KT - 1))
                    mm.then_inc(wide_made, 1)
                if kt < TILES - 1:
                    turn(t + 1, kt + 1, kt == 0)
                if kt > 0:
                    shared_down(t - 1, kt - 1, 1 - p)
                pe.wait_ge(chosen_set, t + 1)
                if kt > 0:
                    pe.wait_ge(place_read, t)
                pe.matmul(place, before[:], chosen[p][:], start=True, stop=False)
                pe.matmul(place, ones[:], so_far[p][:], start=False, stop=True).then_inc(place_made, 1)

            turn(0, 0, True)
            pe.wait_ge(weights_in[0], 32)
            pe.wait_ge(consts_set, 3)
            over_tiles(pe, tile)
            shared_down(TILES - 1, TILES - 1, 1)

            def turn_tokens(e, ke, r):
                p = r % 2
                pe.wait_ge(gx_in[r], 16 // RING * (e - r) + 16)
                if ke >= 2:
                    pe.wait_ge(gxT_set, e - 1)
                for k in range(KT):
                    mm = pe.transpose(tp[p][:, k, :], gx[r][:].rearrange("c (h t) -> c t h", t=KT)[:, k, :], ident[:])
                mm.then_inc(gx_turned, 1)

            def out_of(e, ke, r):
                p = r % 2
                pe.wait_ge(hx_set, e + 1)
                if ke >= 2:
                    pe.wait_ge(eo_set, e - 1)
                pe.matmul(down[p][:], hx[p][:, 0, :], w2[r][:, 0, :], start=True, stop=False)
                pe.matmul(down[p][:], hx[p][128 - REST:128, 1, :], w2[r][128 - REST:128, 1, :],
                          start=False, stop=True).then_inc(out_made, 1)

            def expert(e, ke, r):
                p = r % 2
                pe.wait_ge(experts_in[r], 48 // RING * (e - r) + 48)
                pe.wait_ge(gxT_set, e + 1)
                if ke >= 2:
                    pe.wait_ge(hx_set, e - 1)
                for m in range(2 * I_N // 128):
                    for k in range(KT):
                        mm = pe.matmul(wide[p][:, 128 * m:128 * (m + 1)], w1[r][:, k, 128 * m:128 * (m + 1)],
                                       gxT[p][:, k, :], start=(k == 0), stop=(k == KT - 1))
                mm.then_inc(both_made, 1)
                if ke < E_N - 1:
                    turn_tokens(e + 1, ke + 1, (r + 1) % RING)
                if ke > 0:
                    out_of(e - 1, ke - 1, (r - 1) % RING)

            pe.wait_ge(added, TILES + 1)
            pe.wait_ge(place_read, TILES)
            turn_tokens(0, 0, 0)
            for e in range(RING):
                expert(e, e, e)
            with pe.Fori(1, E_N // RING - 1) as i:
                for r in range(RING):
                    expert(RING * i + r, RING + r, r)
            for r in range(RING):
                expert(E_N - RING + r, E_N - RING + r, r)
            out_of(E_N - 1, E_N - 1, RING - 1)

        @block.scalar
        def _(act):
            def turned_out(t, p):
                act.wait_ge(turned, t + 1)
                nc.scalar.copy(xT[p][:], tp[p][:]).then_inc(xT_set, 1)

            def tile(kt, t):
                p = kt % 2
                act.wait_ge(nmax_set, t + 1)
                nc.scalar.activation(ex[:], logits, ACT.Exp, bias=nmax[:], accum_out=total[:])\
                  .then_inc(ex_set, 1)
                act.wait_ge(wide_made, 2 * t + 1)
                if kt > 0:
                    act.wait_ge(hid_set, t)
                nc.scalar.activation(silu[:], wide[0][:, 0:SI], ACT.Silu).then_inc(silu_set, 1)
                if kt < TILES - 1:
                    if kt > 0:
                        act.wait_ge(wide_made, 2 * t)
                    turned_out(t + 1, 1 - p)

            norm.roots(act, 0, slice(0, TILES))
            turned_out(0, 0)
            over_tiles(act, tile)

            def tokens_out(e, ke, p):
                act.wait_ge(gx_turned, e + 1)
                if ke >= 2:
                    act.wait_ge(both_made, e - 1)
                nc.scalar.copy(gxT[p][:], tp[p][:]).then_inc(gxT_set, 1)

            def expert(e, ke, p):
                act.wait_ge(both_made, e + 1)
                if ke > 0:
                    act.wait_ge(hx_set, e)
                nc.scalar.activation(sg[:, 0, :], wide[p][:, 0:128], ACT.Silu).then_inc(sg_set, 1)
                nc.scalar.activation(sg[128 - REST:128, 1, :], wide[p][0:REST, 256:384], ACT.Silu).then_inc(sg_set, 1)
                if ke < E_N - 1:
                    tokens_out(e + 1, ke + 1, 1 - p)

            tokens_out(0, 0, 0)
            for e in range(2):
                expert(e, e, e)
            with act.Fori(1, E_N // 2 - 1) as i:
                for p in range(2):
                    expert(2 * i + p, 2 + p, p)
            for p in range(2):
                expert(E_N - 2 + p, E_N - 2 + p, p)

        @block.vector
        def _(dve):
            chain = Chain(dve, route_chain)
            norm.variances(dve, mem["stats"], 0, slice(0, TILES))
            norm.reciprocals(dve, 0, slice(0, TILES))
            dve.sem_inc(added, 1)

            def normalise(t, kt):
                n = kt % AHEAD
                if kt >= AHEAD:
                    dve.wait_ge(turned, t - AHEAD + 1)
                    dve.wait_ge(scattered[n], 16 // AHEAD * TOP * (t - n))
                dve.tensor_scalar(xl[n][:], X[:, t, :], norm.mean_of(t), norm.rstd_of(t),
                                  ALU.subtract, ALU.mult).then_inc(xl_set, 1)

            def add_shared(t, p):
                dve.wait_ge(down_made, t + 1)
                dve.tensor_tensor(X[:, t, :], down[p][:], X[:, t, :], ALU.add).then_inc(added, 1)

            def tile(kt, t):
                p = kt % 2
                chain.base, chain.n = 3 + ROUTE_OPS * t, 0
                dve.wait_ge(logits_made, t + 1)
                dve.tensor_reduce(nmax[:], logits, AX.X, ALU.max, negate=True).then_inc(nmax_set, 1)
                if kt < TILES - 1:
                    normalise(t + 1, kt + 1)
                dve.wait_ge(ex_set, t + 1)
                chain(dve.reciprocal(rtotal[:], total[:]))
                chain(dve.tensor_scalar(pp[:, 0:E_N], ex[:], rtotal[:], None, ALU.mult))
                own(dve)
                chain(dve.max(best[:], pp[:]))
                chain(dve.memset(best[:, TOP:8], -1.0))
                own(dve)
                chain(dve.match_replace(left[:], best[:], pp[:], -2.0))
                if kt >= 2:
                    dve.wait_ge(place_made, t - 1)
                chain(dve.tensor_scalar(chosen[p][:], left[:, 0:E_N], -2.0, None, ALU.is_equal))
                dve.tensor_tensor(so_far[1 - p][:], so_far[p][:], chosen[p][:], ALU.add).then_inc(chosen_set, 1)
                chain(dve.tensor_tensor(weight[:], pp[:, 0:E_N], chosen[p][:], ALU.mult))
                dve.wait_ge(silu_set, t + 1)
                dve.wait_ge(wide_made, 2 * t + 2)
                if kt >= 2:
                    dve.wait_ge(down_made, t - 1)
                dve.tensor_tensor(hid[p][:], wide[1][:, 0:SI], silu[:], ALU.mult).then_inc(hid_set, 1)
                if kt > 0:
                    add_shared(t - 1, 1 - p)
                dve.wait_ge(place_made, t + 1)
                chain(dve.scalar_tensor_tensor(kept[:], place, float(CAP), chosen[p][:], ALU.is_lt, ALU.mult))
                chain(dve.tensor_tensor(slot[:], place, first_slot[:], ALU.add))
                dve.sem_inc(place_read, 1)
                chain(dve.tensor_tensor(slot[:], slot[:], kept[:], ALU.mult))
                chain(dve.tensor_tensor(weight[:], weight[:], kept[:], ALU.mult))
                own(dve)
                chain(dve.max(slots8[:], slot[:]))
                chain(dve.tensor_scalar(dropped[:], slots8[:], 0.0, float(SLOTS + 1), ALU.is_equal, ALU.mult))
                chain(dve.scalar_tensor_tensor(dropped[:], slots8[:], -1.0, dropped[:], ALU.add, ALU.add))
                n = kt % AHEAD
                if kt >= AHEAD:
                    dve.wait_ge(scattered[n], 16 // AHEAD * TOP * (t - n))
                dve.tensor_copy(index[n][:], dropped[:]).then_inc(index_set, 1)
                chain(dve.tensor_copy(all_index[:, t, :], dropped[:]))
                for k in range(TOP):
                    chain(dve.scalar_tensor_tensor(matches[:, k, :], slot[:], slots8[:, k:k + 1], weight[:],
                                                   ALU.is_equal, ALU.mult))
                chain(dve.tensor_reduce(all_weight[:, t, 0:TOP], matches[:], AX.X, ALU.add))
                assert chain.n == ROUTE_OPS, chain.n

            chain(dve.memset(pp[:, E_N:E_N + 8], -1.0))
            chain(dve.memset(so_far[0][:], 0.0))
            dve.wait_ge(consts_set, 3)
            chain(dve.tensor_copy(first_slot[:], first_slot_i[:]))
            normalise(0, 0)
            over_tiles(dve, tile)
            add_shared(TILES - 1, 1)

            def expert_out(e, ke, p):
                dve.wait_ge(out_made, e + 1)
                if ke >= 2:
                    dve.wait_ge(eo_stored[p], 8 * (e - p))
                dve.tensor_copy(eo[p][:], down[p][:]).then_inc(eo_set, 1)

            def expert(e, ke, p):
                dve.wait_ge(sg_set, 2 * e + 2)
                if ke >= 2:
                    dve.wait_ge(out_made, e - 1)
                dve.tensor_tensor(hx[p][:, 0, :], wide[p][:, 128:256], sg[:, 0, :], ALU.mult)
                rest = slice(128 - REST, 128)
                dve.tensor_tensor(hx[p][rest, 1, :], wide[p][rest, 256:384], sg[rest, 1, :], ALU.mult)\
                   .then_inc(hx_set, 1)
                if ke > 0:
                    expert_out(e - 1, ke - 1, 1 - p)

            for e in range(3):
                expert(e, e, e % 2)
            with dve.Fori(1, E_N // 2 - 1) as i:
                for p in range(2):
                    expert(2 * i + 1 + p, 3 + p, 1 - p)
            expert(E_N - 1, E_N - 1, 1)
            expert_out(E_N - 1, E_N - 1, 1)

        @block.gpsimd
        def _(pool):
            pool.memset(ones[:], 1.0).then_inc(consts_set, 1)
            pool.wait_ge(consts_set, 1)
            pool.affine_select(out=before[:], in_=ones[:], compare_op=ALU.is_gt, fill=0.0, base=0,
                               pattern=[[1, 128]], channel_multiplier=-1).then_inc(consts_set, 1)
            pool.iota(first_slot_i[:], pattern=[[CAP, E_N]], base=1, channel_multiplier=0).then_inc(consts_set, 1)
            pool.wait_ge(mem["zeroed"], 16 * (4 * B + 1))

            def scatter(t, n):
                pool.wait_ge(index_set, t + 1)
                own(pool)
                for k in range(TOP):
                    pool.indirect_dma_start(out=slot_rows, out_offset=bass.IndirectOffsetOnAxis(
                        index[n][:, k:k + 1].bitcast(U32), 0), in_=xl[n][:], in_offset=None,
                        bounds_check=SLOTS - 1, oob_is_err=False).then_inc(scattered[n], 16)

            with pool.Fori(0, TILES // AHEAD) as i:
                for n in range(AHEAD):
                    scatter(AHEAD * i + n, n)


R_N, R_TOP = 8, 2


def routed_sum(nc, d, X, mem, out):
    ident = mem["ident"]
    with ExitStack() as ctx:
        def sb(name, shape, dt):
            return ctx.enter_context(nc.sbuf_tensor("m1" + name, shape, dt))

        def pb(name, shape, dt):
            return ctx.enter_context(nc.psum_tensor("m1" + name, shape, dt))

        def sem(name):
            return ctx.enter_context(nc.semaphore("m1" + name))

        w1, w3, w2 = (sb(n, [128, KT, N], F32) for n in ("w1", "w3", "w2"))
        wr = sb("wr", [128, KT, R_N], F32)
        xl = [sb(f"xl{p}", [128, N], F32) for p in range(2)]
        xT = [sb(f"xT{p}", [128, KT, 128], F32) for p in range(2)]
        h1 = [sb(f"h1{p}", [128, KT, 128], F32) for p in range(2)]
        h2 = [sb(f"h2{p}", [128, N], F32) for p in range(2)]
        nmax, total, rtotal, gsum = (sb(n, [128, 1], F32) for n in ("nmax", "total", "rtotal", "gsum"))
        ex = sb("ex", [128, R_N], F32)
        pp, left = sb("pp", [128, 2 * R_N], F32), sb("left", [128, 2 * R_N], F32)
        best = sb("best", [128, 8], F32)
        gates = [sb(f"gates{p}", [128, R_N], F32) for p in range(2)]
        summed = sb("summed", [R_N, N], F32)
        summedT = sb("summedT", [128, KT, R_N], F32)

        tp = [pb(f"tp{p}", [128, KT, 128], F32) for p in range(2)]
        first = [pb(f"first{p}", [128, KT, 128], F32) for p in range(2)]
        second = [pb(f"second{p}", [128, N], F32) for p in range(2)]
        small = pb("small", [128, N], F32)
        acc = pb("acc", [R_N, N], F32)

        weights_in = [sem(f"weights_in{n}") for n in range(2)]
        xl_set, turned, xT_set = sem("xl_set"), sem("turned"), sem("xT_set")
        logits_made, nmax_set, ex_set, gates_set = sem("logits_made"), sem("nmax_set"), sem("ex_set"), sem("gates_set")
        first_made, h1_set, second_made, h2_set = sem("first_made"), sem("h1_set"), sem("second_made"), sem("h2_set")
        gathered = sem("gathered")
        summed_set, summed_turned, summedT_set, last_made = (
            sem(n) for n in ("summed_set", "summed_turned", "summedT_set", "last_made"))
        gate_chain = sem("gate_chain")
        x_out = sem("x_out")
        def own(engine):
            engine.sem_inc(mem["passed"], 1)

        norm = Moments(nc, ctx, "m1", mem, TILES, 1)
        GATE_OPS = 9
        block = ctx.enter_context(nc.Block())

        def over_tiles(eng, tile):
            for t in range(2):
                tile(t, t)
            with eng.Fori(1, TILES // 2 - 1) as i:
                for p in range(2):
                    tile(2 + p, 2 * i + p)
            for t in range(TILES - 2, TILES):
                tile(t, t)

        @block.sync
        def _(sp):
            for n, t, name in ((0, wr, "wr"), (0, w1, "w1"), (1, w3, "w3"), (1, w2, "w2")):
                sp.dma_start(t[:], d[name]).then_inc(weights_in[n], 16)
            for b in range(1, B):
                sp.dma_start(out[b].rearrange("(t p) n -> p t n", p=128), X[:, CT * b:CT * (b + 1), :])\
                  .then_inc(x_out, 16)
            sp.wait_ge(gate_chain, GATE_OPS * TILES + 2)
            sp.dma_start(out[0].rearrange("(t p) n -> p t n", p=128), X[:, 0:CT, :]).then_inc(x_out, 16)
            sp.wait_ge(x_out, 16 * B)

        @block.tensor
        def _(pe):
            def turn(t, kt, p):
                pe.wait_ge(xl_set, t + 1)
                if kt >= 2:
                    pe.wait_ge(xT_set, t - 1)
                for k in range(KT):
                    mm = pe.transpose(tp[p][:, k, :], xl[p][:, 128 * k:128 * (k + 1)], ident[:])
                mm.then_inc(turned, 1)

            def second_of(t, kt, p):
                pe.wait_ge(h1_set, t + 1)
                if kt >= 2:
                    pe.wait_ge(h2_set, t - 1)
                for k in range(KT):
                    mm = pe.matmul(second[p][:], h1[p][:, k, :], w3[:, k, :], start=(k == 0), stop=(k == KT - 1))
                mm.then_inc(second_made, 1)

            def gather(t, p, start, stop):
                pe.wait_ge(h2_set, t + 1)
                pe.wait_ge(gates_set, t + 1)
                pe.matmul(acc[:], gates[p][:], h2[p][:], start=start, stop=stop).then_inc(gathered, 1)

            def tile(kt, t):
                p = kt % 2
                pe.wait_ge(xT_set, t + 1)
                if kt > 0:
                    pe.wait_ge(ex_set, t)
                for k in range(KT):
                    mm = pe.matmul(small[:, 0:R_N], xT[p][:, k, :], wr[:, k, :], start=(k == 0), stop=(k == KT - 1))
                mm.then_inc(logits_made, 1)
                if kt >= 2:
                    pe.wait_ge(h1_set, t - 1)
                for m in range(KT):
                    for k in range(KT):
                        mm = pe.matmul(first[p][:, m, :], w1[:, k, 128 * m:128 * (m + 1)], xT[p][:, k, :],
                                       start=(k == 0), stop=(k == KT - 1))
                mm.then_inc(first_made, 1)
                if kt < TILES - 1:
                    turn(t + 1, kt + 1, 1 - p)
                if kt == 1:
                    pe.wait_ge(weights_in[1], 32)
                if kt >= 1:
                    second_of(t - 1, kt - 1, 1 - p)
                if kt >= 2:
                    gather(t - 2, p, kt == 2, False)

            turn(0, 0, 0)
            pe.wait_ge(weights_in[0], 32)
            for t in range(3):
                tile(t, t)
            with pe.Fori(1, TILES // 2 - 1) as i:
                for p in range(2):
                    tile(3 + p, 2 * i + 1 + p)
            tile(TILES - 1, TILES - 1)
            second_of(TILES - 1, TILES - 1, 1)
            gather(TILES - 2, 0, False, False)
            gather(TILES - 1, 1, False, True)
            pe.wait_ge(summed_set, 1)
            for k in range(KT):
                mm = pe.transpose(small[:, 64 + R_N * k:64 + R_N * (k + 1)], summed[:, 128 * k:128 * (k + 1)],
                                  ident[0:R_N, 0:R_N])
            mm.then_inc(summed_turned, 1)
            pe.wait_ge(summedT_set, 1)
            for k in range(KT):
                mm = pe.matmul(acc[:], summedT[:, k, :], w2[:, k, :], start=(k == 0), stop=(k == KT - 1))
            mm.then_inc(last_made, 1)

        @block.scalar
        def _(act):
            def turned_out(t, kt, p):
                act.wait_ge(turned, t + 1)
                if kt >= 2:
                    act.wait_ge(first_made, t - 1)
                nc.scalar.copy(xT[p][:], tp[p][:]).then_inc(xT_set, 1)

            def second_out(t, kt, p):
                act.wait_ge(second_made, t + 1)
                if kt >= 2:
                    act.wait_ge(gathered, t - 1)
                nc.scalar.activation(h2[p][:], second[p][:], ACT.Silu).then_inc(h2_set, 1)

            def tile(kt, t):
                p = kt % 2
                act.wait_ge(nmax_set, t + 1)
                nc.scalar.activation(ex[:], small[:, 0:R_N], ACT.Exp, bias=nmax[:], accum_out=total[:])\
                  .then_inc(ex_set, 1)
                act.wait_ge(first_made, t + 1)
                if kt >= 2:
                    act.wait_ge(second_made, t - 1)
                nc.scalar.activation(h1[p][:], first[p][:], ACT.Silu).then_inc(h1_set, 1)
                if kt < TILES - 1:
                    turned_out(t + 1, kt + 1, 1 - p)
                if kt >= 1:
                    second_out(t - 1, kt - 1, 1 - p)

            norm.roots(act, 0, slice(0, TILES))
            turned_out(0, 0, 0)
            for t in range(3):
                tile(t, t)
            with act.Fori(1, TILES // 2 - 1) as i:
                for p in range(2):
                    tile(3 + p, 2 * i + 1 + p)
            tile(TILES - 1, TILES - 1)
            second_out(TILES - 1, TILES - 1, 1)

        @block.vector
        def _(dve):
            norm.variances(dve, mem["stats"], 0, slice(0, TILES))
            norm.reciprocals(dve, 0, slice(0, TILES))
            chain = Chain(dve, gate_chain)

            def normalise(t, kt, p):
                if kt >= 2:
                    dve.wait_ge(turned, t - 1)
                dve.tensor_scalar(xl[p][:], X[:, t, :], norm.mean_of(t), norm.rstd_of(t),
                                  ALU.subtract, ALU.mult).then_inc(xl_set, 1)

            def tile(kt, t):
                p = kt % 2
                chain.base, chain.n = 1 + GATE_OPS * t, 0
                dve.wait_ge(logits_made, t + 1)
                dve.tensor_reduce(nmax[:], small[:, 0:R_N], AX.X, ALU.max, negate=True).then_inc(nmax_set, 1)
                if kt < TILES - 1:
                    normalise(t + 1, kt + 1, 1 - p)
                dve.wait_ge(ex_set, t + 1)
                chain(dve.reciprocal(rtotal[:], total[:]))
                chain(dve.tensor_scalar(pp[:, 0:R_N], ex[:], rtotal[:], None, ALU.mult))
                own(dve)
                chain(dve.max(best[:], pp[:]))
                chain(dve.memset(best[:, R_TOP:8], -1.0))
                own(dve)
                chain(dve.match_replace(left[:], best[:], pp[:], -2.0))
                chain(dve.tensor_scalar(left[:, 0:R_N], left[:, 0:R_N], -2.0, None, ALU.is_equal))
                chain(dve.tensor_tensor(left[:, 0:R_N], left[:, 0:R_N], pp[:, 0:R_N], ALU.mult))
                chain(dve.tensor_reduce(gsum[:], left[:, 0:R_N], AX.X, ALU.add))
                chain(dve.reciprocal(gsum[:], gsum[:]))
                if kt >= 2:
                    dve.wait_ge(gathered, t - 1)
                dve.tensor_scalar(gates[p][:], left[:, 0:R_N], gsum[:], None, ALU.mult).then_inc(gates_set, 1)
                assert chain.n == GATE_OPS, chain.n

            chain(dve.memset(pp[:, R_N:2 * R_N], -1.0))
            normalise(0, 0, 0)
            over_tiles(dve, tile)
            dve.wait_ge(gathered, TILES)
            dve.tensor_copy(summed[:], acc[:]).then_inc(summed_set, 1)
            dve.wait_ge(summed_turned, 1)
            dve.tensor_copy(summedT[:], small[:, 64:64 + R_N * KT].rearrange("p (k r) -> p k r", k=KT))\
               .then_inc(summedT_set, 1)
            dve.wait_ge(last_made, 1)
            chain.base, chain.n = 1 + GATE_OPS * TILES, 0
            chain(dve.tensor_tensor(X[0:R_N, 0, :], acc[:], X[0:R_N, 0, :], ALU.add))


def program(nc, d, out):
    with ExitStack() as ctx:
        X = ctx.enter_context(nc.sbuf_tensor("X", [128, TILES, N], F32))
        mem = {
            "ident": ctx.enter_context(nc.sbuf_tensor("ident", [128, 128], F32)),
            "ident_b": ctx.enter_context(nc.sbuf_tensor("ident_b", [128, 128], BF16)),
            "all_index": ctx.enter_context(nc.sbuf_tensor("all_index", [128, TILES, 8], I32)),
            "all_weight": ctx.enter_context(nc.sbuf_tensor("all_weight", [128, TILES, 8], F32)),
        }
        mem["slot_rows"] = nc.dram_tensor("slot_rows", [SLOTS, N], F32, kind="Internal").ap()
        mem["expert_rows"] = nc.dram_tensor("expert_rows", [SLOTS + 1, N], F32, kind="Internal").ap()
        mem["passed"] = ctx.enter_context(nc.semaphore("passed"))
        mem["zeroed"] = ctx.enter_context(nc.semaphore("zeroed"))
        mem["zero"] = ctx.enter_context(nc.sbuf_tensor("zero", [128, N], F32))
        mem["stats"] = ctx.enter_context(nc.sbuf_tensor("stats", [128, TILES, 6], F32))
        mem["moment_runs"] = 0
        mem["moments_chain"] = ctx.enter_context(nc.semaphore("moments_chain"))
        mem["root_set"] = ctx.enter_context(nc.semaphore("root_set"))
        mem["made"] = ctx.enter_context(nc.semaphore("made"))
        attention(nc, "a0", {**{k: d["L0_" + k] for k in ("wq", "wk", "wv", "wo", "biases")},
                             "ctx": d["ctx_2048"], "enc": d["enc"], "sign": d["sign"]}, X, mem, 0.25,
                  start=loading(nc, ctx, X, mem, d["x"]))
        mixture(nc, d, X, mem)
        attention(nc, "a1", {**{k: d["L1_" + k] for k in ("wq", "wk", "wv", "wo", "biases")},
                             "ctx": d["ctx_2048"]}, X, mem, 0.25)
        routed_sum(nc, d, X, mem, out)


def laid_out(inputs):
    import numpy as np

    a = {k: np.asarray(v) for k, v in inputs.items()}

    def tiles(w):
        return np.ascontiguousarray(w.reshape(-1, 128, w.shape[1]).transpose(1, 0, 2))

    def by_head(w):
        return w.reshape(HD, H, *w.shape[1:]).swapaxes(0, 1).reshape(w.shape)

    d = {"x": a["x"], "ctx_2048": a["ctx_2048"]}
    for layer, last, order in (("L0", "m", by_head), ("L1", "o", lambda w: w)):
        for n in "qkv":
            d[f"{layer}_w{n}"] = tiles(order(a[f"{layer}_xattn_W{n}"]).T)
        d[f"{layer}_wo"] = tiles(order(a[f"{layer}_xattn_W{last}"].T))
        vectors = [order(a[f"{layer}_xattn_b{n}"]) for n in "qkv"] + [a[f"{layer}_xattn_b{last}"]]
        d[f"{layer}_biases"] = np.ascontiguousarray(np.stack([v.reshape(CT, 128) for v in vectors]).transpose(2, 0, 1))
    d["enc"] = np.ascontiguousarray(a["L0_xattn_encoding"][:, 0, 0].transpose(0, 2, 1))
    d["sign"] = np.where(np.arange(128) % 2 == 0, -1.0, 1.0).astype(np.float32).reshape(128, 1)
    d["gate_w"] = tiles(a["L0_ffn_gate_w"].T)
    gate_up = a["L0_ffn_gate_up_proj"]
    d["gate_up"] = np.concatenate([gate_up[:, :, 0:128], gate_up[:, :, I_N:I_N + 128],
                                   gate_up[:, :, 128:I_N], gate_up[:, :, I_N + 128:]], axis=2)
    d["down"] = a["L0_ffn_down_proj"]
    d["shared_gate"] = tiles(a["L0_ffn_shared_gate_w"].T)
    d["shared_up"] = tiles(a["L0_ffn_shared_up_w"].T)
    d["shared_down"] = tiles(a["L0_ffn_shared_down_w"].T)
    d["w1"] = tiles(a["L1_ffn_w1"].T)
    d["w3"] = tiles(a["L1_ffn_w3"].T)
    d["w2"] = tiles(a["L1_ffn_w2"].T)
    d["wr"] = tiles(a["L1_ffn_wr"].T)
    return d


def kernel(**inputs):
    import concourse.bacc as bacc
    from concourse.bass_utils import run_bass_kernel_spmd

    nc = bacc.Bacc("TRN2", target_bir_lowering=False, num_devices=1)
    arrays, aps = {}, {}
    for name, a in laid_out(inputs).items():
        arrays[f"in_{name}"] = a
        aps[name] = nc.dram_tensor(f"in_{name}", a.shape, mybir.dt.from_np(a.dtype), kind="ExternalInput").ap()
    out = nc.dram_tensor("out_rows", (B, C, N), F32, kind="ExternalOutput").ap()
    program(nc, aps, out)
    r = run_bass_kernel_spmd(nc, [arrays], core_ids=[0])
    return r.results[0]["out_rows"]
```
